# Optimizing a Trainium2 kernel written in Bass

```python
import numpy as np
import jax
import jax.numpy as jnp

def _softmax(x, axis=-1):
    return jax.nn.softmax(x, axis=axis)

def _gelu(x):
    return jax.nn.gelu(x, approximate=True)

def _silu(x):
    return jax.nn.silu(x)

def _sigmoid(x):
    return jax.nn.sigmoid(x)

def _layernorm(x, axis=-1, eps=1e-05):
    m = jnp.mean(x, axis=axis, keepdims=True)
    v = jnp.var(x, axis=axis, keepdims=True)
    return (x - m) / jnp.sqrt(v + eps)

def _scatter_add(tgt, idx, src, axis=0):
    return tgt.at[idx].add(src)

def _segment_sum(src, seg, n):
    return jax.ops.segment_sum(src, seg, n)
kernel_name = 'mk_gnn_resnorm_d4_gnn_r8_37a730'

def setup_inputs(seed: int=0):
    np.random.seed(seed)
    _w = jnp.asarray

    def _rec_inputs():
        import jax
        import jax.numpy as jnp
        _gk = jax.random.key(seed)
        x = -0.0005121 + 1.001 * jax.random.normal(jax.random.fold_in(_gk, 1), (6250, 64), jnp.float32)
        _s = jax.random.randint(jax.random.fold_in(_gk, 2), (100000,), 0, 6250, jnp.int32)
        _d = jax.random.randint(jax.random.fold_in(_gk, 3), (100000,), 0, 6250, jnp.int32)
        _loop = jnp.arange(6250, dtype=jnp.int32)
        src = jnp.concatenate([_s, _d, _loop])
        dst = jnp.concatenate([_d, _s, _loop])
        _o = jnp.argsort(dst, stable=True)
        src = src[_o]
        dst = dst[_o]
        edge_attr_32 = 0.000196303 + 1.00016 * jax.random.normal(jax.random.fold_in(_gk, 12), (206250, 32), jnp.float32)
        edge_weight = jax.random.uniform(jax.random.fold_in(_gk, 14), (206250,), jnp.float32, 0.0, 0.999999)
        return (x, src, dst, edge_attr_32, edge_weight)
    x, src, dst, edge_attr_32, edge_weight = _rec_inputs()

    def _L0_gnn_setup():
        import jax, jax.numpy as jnp
        import numpy as np
        N_NODES = 6250
        N_EDGES = 100000
        D = 64
        key = jax.random.key(seed)
        k1, k2, k3, k4, k5 = jax.random.split(key, 5)
        scale = (6.0 / (D + D)) ** 0.5
        return {'feat': jax.random.normal(k1, (N_NODES, D), dtype=jnp.float32), 'Wm': jax.random.uniform(k2, (D, D), dtype=jnp.float32, minval=-scale, maxval=scale), 'bm': jnp.zeros((D,), dtype=jnp.float32), 'Wn': jax.random.uniform(k3, (D, D), dtype=jnp.float32, minval=-scale, maxval=scale), 'bn': jnp.zeros((D,), dtype=jnp.float32), 'src': jax.random.randint(k4, (N_EDGES,), 0, N_NODES, dtype=jnp.int32), 'dst': jax.random.randint(k5, (N_EDGES,), 0, N_NODES, dtype=jnp.int32)}
    _L0_gnn_all = _L0_gnn_setup()
    _L0_gnn_in = {k: v for k, v in _L0_gnn_all.items() if k in ('Wm', 'bm', 'Wn', 'bn')}
    del _L0_gnn_all

    def _L1_gnn_setup():
        import jax, jax.numpy as jnp
        import numpy as np
        N_NODES = 12500
        N_EDGES = 125000
        HIDDEN = 64
        LN_EPS = 1e-08
        key = jax.random.key(seed)
        k1, k2, k3, k4 = jax.random.split(key, 4)
        x = jax.random.normal(k1, (N_NODES, HIDDEN), dtype=jnp.float32)
        edge_index = jax.random.randint(k2, (2, N_EDGES), 0, N_NODES, dtype=jnp.int64)
        W = jax.random.normal(k3, (HIDDEN, HIDDEN), dtype=jnp.float32) / np.sqrt(HIDDEN)
        b = jnp.zeros((HIDDEN,), dtype=jnp.float32)
        ln_gamma = jnp.ones((HIDDEN,), dtype=jnp.float32)
        ln_beta = jnp.zeros((HIDDEN,), dtype=jnp.float32)
        return {'x': x, 'edge_index': edge_index, 'W': W, 'b': b, 'ln_gamma': ln_gamma, 'ln_beta': ln_beta}
    _L1_gnn_all = _L1_gnn_setup()
    _L1_gnn_in = {k: v for k, v in _L1_gnn_all.items() if k in ('W', 'b', 'ln_gamma', 'ln_beta')}
    del _L1_gnn_all

    def _L2_gnn_setup():
        import jax, jax.numpy as jnp
        import numpy as np
        N_NODES = 12500
        N_EDGES = 150000
        D_IN = 64
        D_HID = 64

        def _gcn_conv(x, edge_index, edge_weight, W, b):
            n = x.shape[0]
            loop = jnp.arange(n, dtype=edge_index.dtype)
            row = jnp.concatenate([edge_index[0], loop])
            col = jnp.concatenate([edge_index[1], loop])
            ew = jnp.concatenate([edge_weight, jnp.ones((n,), edge_weight.dtype)])
            deg = jax.ops.segment_sum(ew, col, num_segments=n)
            dis = jnp.where(deg > 0, jax.lax.rsqrt(deg), 0.0)
            norm = dis[row] * ew * dis[col]
            h = x @ W.T
            msg = norm[:, None] * h[row]
            out = jax.ops.segment_sum(msg, col, num_segments=n)
            return out + b
        key = jax.random.key(seed)
        k1, k2, k3, k4 = jax.random.split(key, 4)
        x = jax.random.normal(k1, (N_NODES, D_IN), dtype=jnp.float32)
        edge_index = jax.random.randint(k2, (2, N_EDGES), 0, N_NODES, dtype=jnp.int32)
        edge_attr = jax.random.uniform(k3, (N_EDGES,), dtype=jnp.float32)
        W = jax.random.normal(k4, (D_HID, D_IN), dtype=jnp.float32) / np.sqrt(D_IN)
        b = jnp.zeros((D_HID,), dtype=jnp.float32)
        return {'x': x, 'edge_index': edge_index, 'edge_attr': edge_attr, 'W': W, 'b': b}
    _L2_gnn_all = _L2_gnn_setup()
    _L2_gnn_in = {k: v for k, v in _L2_gnn_all.items() if k in ('W', 'b')}
    del _L2_gnn_all

    def _L3_gnn_setup():
        import jax, jax.numpy as jnp
        import numpy as np
        N, E, H, ED = (6250, 100000, 64, 32)

        def _layernorm(h, gamma, beta, eps=1e-05):
            mu = jnp.mean(h, axis=-1, keepdims=True)
            var = jnp.mean(jnp.square(h - mu), axis=-1, keepdims=True)
            return (h - mu) * jax.lax.rsqrt(var + eps) * gamma + beta
        key = jax.random.key(seed)
        ks = jax.random.split(key, 16)
        s = lambda fan_in: 1.0 / np.sqrt(fan_in)
        inp = {'x': jax.random.normal(ks[0], (N, H), dtype=jnp.float32), 'edge_index': jax.random.randint(ks[1], (2, E), 0, N, dtype=jnp.int64), 'edge_attr': jax.random.normal(ks[2], (E, ED), dtype=jnp.float32), 'w1': jax.random.uniform(ks[3], (2 * H + ED, H), jnp.float32, -s(2 * H + ED), s(2 * H + ED)), 'b1': jnp.zeros((H,), jnp.float32), 'w2': jax.random.uniform(ks[4], (H, H), jnp.float32, -s(H), s(H)), 'b2': jnp.zeros((H,), jnp.float32), 'w3': jax.random.uniform(ks[5], (2 * H, H), jnp.float32, -s(2 * H), s(2 * H)), 'b3': jnp.zeros((H,), jnp.float32), 'w4': jax.random.uniform(ks[6], (H, H), jnp.float32, -s(H), s(H)), 'b4': jnp.zeros((H,), jnp.float32), 'gamma': jnp.ones((H,), jnp.float32), 'beta': jnp.zeros((H,), jnp.float32)}
        return inp
    _L3_gnn_all = _L3_gnn_setup()
    _L3_gnn_in = {k: v for k, v in _L3_gnn_all.items() if k in ('w1', 'b1', 'w2', 'b2', 'w3', 'b3', 'w4', 'b4', 'gamma', 'beta')}
    del _L3_gnn_all
    return {'x': x, 'src': src, 'dst': dst, 'edge_attr_32': edge_attr_32, 'edge_weight': edge_weight, 'L0_gnn_Wm': _L0_gnn_in['Wm'], 'L0_gnn_bm': _L0_gnn_in['bm'], 'L0_gnn_Wn': _L0_gnn_in['Wn'], 'L0_gnn_bn': _L0_gnn_in['bn'], 'L1_gnn_W': _L1_gnn_in['W'], 'L1_gnn_b': _L1_gnn_in['b'], 'L1_gnn_ln_gamma': _L1_gnn_in['ln_gamma'], 'L1_gnn_ln_beta': _L1_gnn_in['ln_beta'], 'L2_gnn_W': _L2_gnn_in['W'], 'L2_gnn_b': _L2_gnn_in['b'], 'L3_gnn_w1': _L3_gnn_in['w1'], 'L3_gnn_b1': _L3_gnn_in['b1'], 'L3_gnn_w2': _L3_gnn_in['w2'], 'L3_gnn_b2': _L3_gnn_in['b2'], 'L3_gnn_w3': _L3_gnn_in['w3'], 'L3_gnn_b3': _L3_gnn_in['b3'], 'L3_gnn_w4': _L3_gnn_in['w4'], 'L3_gnn_b4': _L3_gnn_in['b4'], 'L3_gnn_gamma': _L3_gnn_in['gamma'], 'L3_gnn_beta': _L3_gnn_in['beta']}

def reference(x, src, dst, edge_attr_32, edge_weight, L0_gnn_Wm, L0_gnn_bm, L0_gnn_Wn, L0_gnn_bn, L1_gnn_W, L1_gnn_b, L1_gnn_ln_gamma, L1_gnn_ln_beta, L2_gnn_W, L2_gnn_b, L3_gnn_w1, L3_gnn_b1, L3_gnn_w2, L3_gnn_b2, L3_gnn_w3, L3_gnn_b3, L3_gnn_w4, L3_gnn_b4, L3_gnn_gamma, L3_gnn_beta):
    import jax
    import jax.numpy as jnp

    def _L0_gnn_ref(feat, Wm, bm, Wn, bn, src, dst):
        import jax, jax.numpy as jnp
        import numpy as np
        N_NODES = 6250
        N_EDGES = 100000
        D = 64
        n = feat.shape[0]
        ones = jnp.ones(src.shape[0], dtype=feat.dtype)
        deg_out = jnp.clip(jax.ops.segment_sum(ones, src, num_segments=n), 1.0, None)
        deg_in = jnp.clip(jax.ops.segment_sum(ones, dst, num_segments=n), 1.0, None)
        feat_src = feat * (deg_out ** (-0.5))[:, None]
        e = feat_src[src] * feat[dst]
        e_trans = e @ Wm.T + bm
        u_trans = feat_src @ Wn.T + bn
        msg = u_trans[src] + e_trans
        h = jax.ops.segment_sum(msg, dst, num_segments=n)
        rst = h * (deg_in ** (-0.5))[:, None]
        rst = rst + feat @ Wn.T + bn
        return rst

    def _L1_gnn_ref(x, edge_index, W, b, ln_gamma, ln_beta):
        import jax, jax.numpy as jnp
        import numpy as np
        N_NODES = 12500
        N_EDGES = 125000
        HIDDEN = 64
        LN_EPS = 1e-08
        N = x.shape[0]
        loops = jnp.arange(N, dtype=edge_index.dtype)
        src = jnp.concatenate([edge_index[0], loops])
        dst = jnp.concatenate([edge_index[1], loops])
        h = x @ W
        ones = jnp.ones_like(src, dtype=x.dtype)
        deg = jax.ops.segment_sum(ones, dst, num_segments=N)
        deg_inv_sqrt = jnp.where(deg > 0, jax.lax.rsqrt(deg), 0.0)
        norm = deg_inv_sqrt[src] * deg_inv_sqrt[dst]
        msg = h[src] * norm[:, None]
        agg = jax.ops.segment_sum(msg, dst, num_segments=N) + b
        y = jax.nn.relu(agg) + x
        mean = jnp.mean(y, axis=-1, keepdims=True)
        var = jnp.mean(jnp.square(y - mean), axis=-1, keepdims=True)
        y = (y - mean) * jax.lax.rsqrt(var + LN_EPS)
        return y * ln_gamma + ln_beta

    def _L2_gnn_ref(x, edge_index, edge_attr, W, b):
        import jax, jax.numpy as jnp
        import numpy as np
        N_NODES = 12500
        N_EDGES = 150000
        D_IN = 64
        D_HID = 64

        def _gcn_conv(x, edge_index, edge_weight, W, b):
            n = x.shape[0]
            loop = jnp.arange(n, dtype=edge_index.dtype)
            row = jnp.concatenate([edge_index[0], loop])
            col = jnp.concatenate([edge_index[1], loop])
            ew = jnp.concatenate([edge_weight, jnp.ones((n,), edge_weight.dtype)])
            deg = jax.ops.segment_sum(ew, col, num_segments=n)
            dis = jnp.where(deg > 0, jax.lax.rsqrt(deg), 0.0)
            norm = dis[row] * ew * dis[col]
            h = x @ W.T
            msg = norm[:, None] * h[row]
            out = jax.ops.segment_sum(msg, col, num_segments=n)
            return out + b
        h = _gcn_conv(x, edge_index, edge_attr, W, b)
        return jax.nn.relu(h)

    def _L3_gnn_ref(x, edge_index, edge_attr, w1, b1, w2, b2, w3, b3, w4, b4, gamma, beta):
        import jax, jax.numpy as jnp
        import numpy as np
        N, E, H, ED = (6250, 100000, 64, 32)

        def _layernorm(h, gamma, beta, eps=1e-05):
            mu = jnp.mean(h, axis=-1, keepdims=True)
            var = jnp.mean(jnp.square(h - mu), axis=-1, keepdims=True)
            return (h - mu) * jax.lax.rsqrt(var + eps) * gamma + beta
        source, target = (edge_index[0], edge_index[1])
        m_in = jnp.concatenate([x[source], x[target], edge_attr], axis=-1)
        m = jax.nn.silu(m_in @ w1 + b1) @ w2 + b2
        agg = jax.ops.segment_sum(m, target, num_segments=x.shape[0])
        u_in = jnp.concatenate([x, agg], axis=-1)
        upd = jax.nn.silu(u_in @ w3 + b3) @ w4 + b4
        return _layernorm(x + upd, gamma, beta)
    edge_index = jnp.stack([src, dst])
    x = _layernorm(x + _L0_gnn_ref(x, L0_gnn_Wm, L0_gnn_bm, L0_gnn_Wn, L0_gnn_bn, src, dst), axis=-1)
    x = _layernorm(x + _L1_gnn_ref(x, edge_index, L1_gnn_W, L1_gnn_b, L1_gnn_ln_gamma, L1_gnn_ln_beta), axis=-1)
    x = _layernorm(x + _L2_gnn_ref(x, edge_index, edge_weight, L2_gnn_W, L2_gnn_b), axis=-1)
    x = _layernorm(x + _L3_gnn_ref(x, edge_index, edge_attr_32, L3_gnn_w1, L3_gnn_b1, L3_gnn_w2, L3_gnn_b2, L3_gnn_w3, L3_gnn_b3, L3_gnn_w4, L3_gnn_b4, L3_gnn_gamma, L3_gnn_beta), axis=-1)
    return x

_drawn_inputs = setup_inputs


def setup_inputs(seed=0):
    import zlib

    import numpy as np

    out = dict(_drawn_inputs(seed))
    spreads = {'L0_gnn_bm': (0.0, 0.1),
     'L0_gnn_bn': (0.0, 0.1),
     'L1_gnn_b': (0.0, 0.1),
     'L1_gnn_ln_gamma': (1.0, 0.2),
     'L1_gnn_ln_beta': (0.0, 0.1),
     'L2_gnn_b': (0.0, 0.1),
     'L3_gnn_b1': (0.0, 0.1),
     'L3_gnn_b2': (0.0, 0.1),
     'L3_gnn_b3': (0.0, 0.529),
     'L3_gnn_b4': (0.0, 0.1),
     'L3_gnn_gamma': (1.0, 0.2),
     'L3_gnn_beta': (0.0, 0.1)}
    factors = {}
    for name, (base, spread) in spreads.items():
        noise = np.random.default_rng([zlib.crc32(name.encode()), seed]).standard_normal(out[name].shape)
        drawn = base * np.exp(spread * noise) if base else spread * noise
        out[name] = jnp.asarray(drawn.astype(out[name].dtype))
    for name, factor in factors.items():
        out[name] = (out[name] * factor).astype(out[name].dtype)
    return out
```

```python
from contextlib import ExitStack

import concourse.bass as bass
from concourse import mybir

F32 = mybir.dt.float32
BF16 = mybir.dt.bfloat16
I32 = mybir.dt.int32
ALU = mybir.AluOpType
ACT = mybir.ActivationFunctionType
AX = mybir.AxisListType

P = 128
D = 64
DE = 32
TG = 8
GE = P * TG
W = 64
BB = 5
COLS = 16
TINY = 1.1754944e-38


def padded(n, unit):
    return -(-n // unit) * unit


def shapes(n_nodes, n_edges):
    return padded(n_nodes + 1 + W, 2 * BB * P), padded(n_edges, 2 * GE)


WEIGHTS = {}
_at = 0
for _name, _cols in (("edge", 4 * D), ("wn", D + 2), ("wm", D), ("xn", D), ("w1", D), ("w2", D), ("pq", 2 * D),
                     ("w2t_b2", D + 1), ("w3b", D), ("w3a", D), ("w4", D)):
    WEIGHTS[_name] = (_at, _cols)
    _at += _cols
WCOLS = _at
ROWS = {name: k for k, name in enumerate(("b1", "gamma1", "beta1", "b2", "gamma3", "beta3"))}


class Chain:

    def __init__(self, engine, sem):
        self.engine, self.sem, self.done, self.base, self.n, self.per = engine, sem, 0, 0, 0, 0

    def enter(self, i, per):
        self.base, self.n, self.per = self.done + i * per, 0, per

    def leave(self, times):
        assert self.n == self.per, (self.n, self.per)
        self.done += times * self.per
        self.base, self.n = self.done, 0

    def __call__(self, ins):
        self.n += 1
        ins.then_inc(self.sem, 1)
        self.engine.wait_ge(self.sem, self.base + self.n)

    def close(self):
        self.done += self.n
        self.base, self.n = self.done, 0


def gnn_program(nc, x_nodes, x_t, src_cols, dst_cols, dst_first, w_cols, edge_t, weights, rows, out):
    NB = x_nodes.shape[1]
    NP = NB * P
    NG = src_cols.shape[1] // TG
    NW = NP // W
    NBATCH = NB // BB
    BN = BB * P

    ctx = ExitStack()
    with ctx:
        def sb(name, shape, dt=F32):
            return ctx.enter_context(nc.sbuf_tensor(name, shape, dt))

        def ps(name, shape, dt=F32):
            return ctx.enter_context(nc.psum_tensor(name, shape, dt))

        def sem(name):
            return ctx.enter_context(nc.semaphore(name))

        table = [nc.dram_tensor(f"table{n}", (NP, D), F32, kind="Internal").ap() for n in range(4)]
        q_parts_dram = nc.dram_tensor("q_parts_dram", (NP, 3 * D), BF16, kind="Internal").ap()
        q_dram = nc.dram_tensor("q_dram", (NP, D), F32, kind="Internal").ap()

        X = sb("X", [P, NB, D])
        XT = sb("XT", [D, NP])
        accT = sb("accT", [D + 2, NP])
        weight_cols = sb("weight_cols", [P, NG * TG])
        edge_i = sb("edge_i", [P, NG * TG], I32)
        dst_f = sb("dst_f", [P, NG * TG])
        dst_rel = sb("dst_rel", [P, NG * TG])
        src_lo = sb("src_lo", [P, NG * TG], BF16)
        src_hi = sb("src_hi", [P, NG * TG], BF16)
        X0 = sb("X0", [P, NB, D])
        first_i = sb("first_i", [1, NG], I32)
        first_bc = sb("first_bc", [P, NG], I32)
        first_f = sb("first_f", [P, NG])
        Wt = sb("Wt", [P, WCOLS])
        R = sb("R", [P, len(ROWS), D])
        w23 = sb("w23", [D + 1, D])
        ident = sb("ident", [P, P])
        ident16 = sb("ident16", [P, P], BF16)
        iota_i = sb("iota_i", [P, P], I32)
        iota_f = sb("iota_f", [P, P])
        zero16 = sb("zero16", [P, P], BF16)
        degrees = sb("degrees", [P, NB, 2])
        r_out = sb("r_out", [P, NB])
        dinv1 = sb("dinv1", [P, NB])
        dis2 = sb("dis2", [P, NB])
        dis_a = sb("dis_a", [P, NB])
        dis_b = sb("dis_b", [P, NB])
        span = sb("span", [P, 4])
        flag_i = sb("flag_i", [1, 1], I32)
        flag_f = sb("flag_f", [1, 2])

        idx = sb("idx", [P, 2, TG], I32)
        didx = sb("didx", [P, TG], I32)
        msg = sb("msg", [P, 2, TG, D + 2])
        act_in = sb("act_in", [P, 2, TG, D])
        q_rows = sb("q_rows", [P, TG, D])
        edge_sb = sb("edge_sb", [P, 2, 2, P])
        q_win = sb("q_win", [W, 2, 3 * D], BF16)
        onehot = sb("onehot", [P, 2, TG, W])
        onehot16 = sb("onehot16", [P, 2, TG, W], BF16)
        onehot_t = sb("onehot_t", [W, 2, GE], BF16)
        hist_lo = sb("hist_lo", [P, 2, TG, P], BF16)
        hist_hi = sb("hist_hi", [P, 2, TG, NB], BF16)
        rel_w = sb("rel_w", [P, TG])

        s_t = [sb(f"s_t{b}", [D + 2, BN]) for b in range(2)]
        x_tb = [sb(f"x_tb{b}", [D + 1, BN]) for b in range(2)]
        sx_t = [sb(f"sx_t{b}", [D + 1, BN]) for b in range(2)]
        u = [sb(f"u{b}", [P, BB, D]) for b in range(2)]
        tab = [sb(f"tab{b}", [P, BB, D]) for b in range(2)]
        q_f = [sb(f"q_f{b}", [P, BB, D]) for b in range(2)]
        q_s = [sb(f"q_s{b}", [P, BB, 3 * D], BF16) for b in range(2)]
        q_rest = sb("q_rest", [P, BB, D])
        t1 = sb("t1", [P, BB, D])
        t2 = sb("t2", [P, BB, D])
        c1 = sb("c1", [P, BB])
        c2 = sb("c2", [P, 2, BB])
        c3 = sb("c3", [P, 2, BB])
        minus_half = sb("minus_half", [P, NB])

        bank = [ps(f"bank{n}", [P, 512]) for n in range(4)]
        pair = [ps(f"pair{n}", [P, 1024]) for n in range(2)]
        win = [bank[b][:, 0:W] for b in range(2)]
        zed = [bank[2 + b][:, :].rearrange("p (t d) -> p t d", t=TG) for b in range(2)]
        oh_t = [pair[b][0:W, 0:512].bitcast(BF16) for b in range(2)]
        node_a = [bank[2 + b][:, 0:BB * (D + 2)].rearrange("p (k d) -> p k d", k=BB) for b in range(2)]
        node_b = [pair[0][:, 512 * b:512 * b + BB * D].rearrange("p (k d) -> p k d", k=BB) for b in range(2)]
        node_pq = pair[0]
        node_t = pair[1]
        hist = bank[0][:, 0:NB]

        ld_x, ld_src, ld_dst, ld_first, ld_w = (sem(n) for n in ("ld_x", "ld_src", "ld_dst", "ld_first", "ld_w"))
        consts, dve_step, src_split = sem("consts"), sem("dve_step"), sem("src_split")
        hist_oh, hist_mm = sem("hist_oh"), sem("hist_mm")
        span_ready, span_turned, flag_ready = sem("span_ready"), sem("span_turned"), sem("flag_ready")
        w23_mm, w23_ready, t0_ready, cleared = sem("w23_mm"), sem("w23_ready"), sem("t0_ready"), sem("cleared")

        def per_layer(name, layers=range(4)):
            return {n: sem(f"{name}_{n}") for n in layers}

        def per_slot(name, layers=range(4)):
            return {n: [sem(f"{name}_{n}{b}") for b in range(2)] for n in layers}

        idx_in, gathered = per_slot("idx_in"), per_slot("gathered")
        oh_raw = sem("oh_raw")
        oh_ready, win_done, acc_added = per_layer("oh_ready"), per_layer("win_done"), per_layer("acc_added")
        edge_in, q_in = [sem(f"edge_in{b}") for b in range(2)], [sem(f"q_in{b}") for b in range(2)]
        turn_done, turn_copied, zed_done = sem("turn_done"), sem("turn_copied"), sem("zed_done")
        z_summed, silu_done = sem("z_summed"), sem("silu_done")
        g_idx, g_gathered, g_free = per_layer("g_idx"), per_layer("g_gathered"), per_layer("g_free")
        g_rel, g_raw, g_oh = per_layer("g_rel"), sem("g_raw"), per_layer("g_oh")
        g_win, g_added = per_layer("g_win"), per_layer("g_added")
        g_edge, g_zed, g_part, g_sum, g_silu = (sem(n) for n in ("g_edge", "g_zed", "g_part", "g_sum", "g_silu"))
        pass_done = per_layer("pass_done")
        asked, rooted = per_layer("asked", (-1, 0, 1, 2, 3)), per_layer("rooted", (-1, 0, 1, 2, 3))
        staged, products, batch_done = per_layer("staged"), per_layer("products"), per_layer("batch_done")
        turned, turned_copied = per_layer("turned"), per_layer("turned_copied")
        sx_ready, pq_done, pq_read, q_split, q_step = (sem(n) for n in ("sx_ready", "pq_done", "pq_read", "q_split", "q_step"))
        u_done, y_done = sem("u_done"), sem("y_done")
        stored = per_slot("stored")
        stored[4] = [sem(f"stored_4{b}") for b in range(2)]

        slot_stored = per_layer("slot_stored", (1, 2, 3, 4))

        STORES = {1: 1, 2: 1, 3: 3, 4: 1}

        def wt(name, k=D):
            at, cols = WEIGHTS[name]
            return Wt[0:k, at:at + cols]

        def row(name, n=BB):
            return R[:, ROWS[name], :].rearrange("p (k d) -> p k d", k=1).broadcast_to((P, n, D))

        def cols(t, g, n=TG):
            return t[:, bass.ds(g * TG, n)]

        def along(ap, n):
            return ap.rearrange("p (k o) -> p k o", o=1).broadcast_to((P, ap.shape[1], n))

        def iota_bc(n, k=TG):
            return iota_f[:, 0:n].rearrange("p (k n) -> p k n", k=1).broadcast_to((P, k, n))

        SUMS = {0: D + 2, 1: D, 2: D, 3: D}
        READ = {0: D + 2, 1: D, 2: D, 3: D + 1}
        ROOTS = {0: 2, 1: 2, 2: 1, 3: 2}

        def skewed(eng, first, second):
            first(0, 0, 0)
            with eng.Fori(0, NBATCH // 2 - 1) as i:
                first(2 * i + 1, 1, i)
                second(2 * i, 0, i)
                first(2 * i + 2, 0, i + 1)
                second(2 * i + 1, 1, i)
            first(NBATCH - 1, 1, NBATCH // 2 - 1)
            second(NBATCH - 2, 0, NBATCH // 2 - 1)
            second(NBATCH - 1, 1, NBATCH // 2 - 1)

        block = ctx.enter_context(nc.Block())

        @block.sync
        def _(sp):
            sp.dma_start(edge_i[:, :], src_cols).then_inc(ld_src, COLS)
            sp.dma_start(first_i[:, :], dst_first[0:1, :]).then_inc(ld_first, COLS)
            sp.dma_start(first_bc[:, :], dst_first).then_inc(ld_first, COLS)
            sp.dma_start(X[:, :, :], x_nodes).then_inc(ld_x, COLS)
            sp.wait_ge(src_split, 1)
            sp.dma_start(edge_i[:, :], dst_cols).then_inc(ld_dst, COLS)
            sp.dma_start(Wt[:, :], weights).then_inc(ld_w, COLS)
            sp.dma_start(R[:, :, :], rows).then_inc(ld_w, COLS)
            sp.dma_start(weight_cols[:, :], w_cols).then_inc(ld_w, COLS)
            sp.dma_start(XT[:, :], x_t).then_inc(ld_w, COLS)
            for n in (1, 2, 3, 4):
                sp.sem_inc(slot_stored[n], 2)
            sp.wait_ge(t0_ready, 1)
            sp.dma_start(table[0].rearrange("(k p) d -> p k d", p=P), X0[:, :, :]).then_inc(stored[0][0], COLS)
            sp.wait_ge(flag_ready, 1)
            spread = sp.value_load(flag_i[0:1, 0:1], min_val=0, max_val=1)

            for layer in range(4):
                if layer == 3:
                    for b in range(2):
                        sp.wait_ge(stored[3][b], COLS * STORES[3] * (NBATCH // 2))
                with sp.If(spread == 0):
                    with sp.Fori(0, NG // 2) as i:
                        for b in range(2):
                            g = 2 * i + b
                            sp.wait_ge(z_summed if layer == 3 else win_done[layer], g + 1)
                            sp.dma_start(idx[:, b, :], cols(src_cols, g)).then_inc(idx_in[layer][b], COLS)
                            if layer == 3:
                                first = sp.value_load(first_i[0:1, bass.ds(g, 1)], min_val=0, max_val=NP - W)
                                sp.wait_ge(zed_done, g + 1)
                                sp.dma_start(edge_sb[:, b, :, :], edge_t[:, bass.ds(g * 2, 2), :])\
                                  .then_inc(edge_in[b], COLS)
                                sp.dma_start(q_win[:, b, :], q_parts_dram[bass.ds(first, W), :])\
                                  .then_inc(q_in[b], COLS)
                with sp.Else():
                    with sp.Fori(0, NG) as g:
                        sp.wait_ge(g_free[layer], g + 1)
                        sp.dma_start(idx[:, 0, :], cols(src_cols, g)).then_inc(g_idx[layer], COLS)
                        if layer == 3:
                            sp.dma_start(didx[:, :], cols(dst_cols, g)).then_inc(g_idx[layer], COLS)
                            sp.wait_ge(g_zed, g + 1)
                            sp.dma_start(edge_sb[:, 0, :, :], edge_t[:, bass.ds(g * 2, 2), :]).then_inc(g_edge, COLS)

                with sp.Fori(0, NBATCH // 2) as i:
                    for b in range(2):
                        j = 2 * i + b
                        of_batch = bass.ds(j * BN, BN)
                        if layer < 2:
                            sp.wait_ge(batch_done[layer], j + 1)
                            sp.dma_start(table[layer + 1][of_batch, :].rearrange("(k p) d -> p k d", p=P),
                                         tab[b][:, :, :]).then_inc(stored[layer + 1][b], COLS)
                        elif layer == 2:
                            sp.wait_ge(pq_read, j + 2)
                            sp.dma_start(table[3][of_batch, :].rearrange("(k p) d -> p k d", p=P),
                                         tab[b][:, :, :]).then_inc(stored[3][b], COLS)
                            sp.dma_start(q_dram[of_batch, :].rearrange("(k p) d -> p k d", p=P),
                                         q_f[b][:, :, :]).then_inc(stored[3][b], COLS)
                            sp.wait_ge(q_split, j + 1)
                            sp.dma_start(q_parts_dram[of_batch, :].rearrange("(k p) d -> p k d", p=P),
                                         q_s[b][:, :, :]).then_inc(stored[3][b], COLS)
                        else:
                            sp.wait_ge(batch_done[3], j + 3)
                            sp.dma_start(out[:, bass.ds(j * BB, BB), :], tab[b][:, :, :]).then_inc(stored[4][b], COLS)
                        sp.wait_ge(stored[layer + 1][b], COLS * STORES[layer + 1] * (i + 1))
                        sp.sem_inc(slot_stored[layer + 1], 1)
            for b in range(2):
                sp.wait_ge(stored[4][b], COLS * (NBATCH // 2))

        @block.gpsimd
        def _(pool):
            pool.memset(ident[:, :], 0.0).then_inc(consts, 1)
            pool.memset(ident16[:, :], 0.0).then_inc(consts, 1)
            pool.iota(iota_i[:, :], pattern=[[1, P]], base=0, channel_multiplier=0).then_inc(consts, 1)
            pool.memset(zero16[:, :], 0.0).then_inc(consts, 1)
            pool.wait_ge(consts, 4)
            for m in (ident, ident16):
                pool.affine_select(out=m[:, :], in_=m[:, :], compare_op=ALU.not_equal, fill=1.0, base=0,
                                   pattern=[[-1, P]], channel_multiplier=1).then_inc(consts, 1)
            pool.memset(minus_half[:, :], -0.5).then_inc(cleared, 1)
            pool.memset(msg[:, :, :, :], 1.0).then_inc(cleared, 1)
            pool.memset(accT[:, :], 0.0).then_inc(cleared, 1)
            pool.wait_ge(cleared, 7)
            pool.wait_ge(asked[-1], 1)
            pool.tensor_tensor(r_out[:, :], r_out[:, :], minus_half[:, :], ALU.pow).then_inc(rooted[-1], 1)
            pool.wait_ge(flag_ready, 1)
            spread = pool.value_load(flag_i[0:1, 0:1], min_val=0, max_val=1)

            def gather(buf, rows_of, at, done):
                for t in range(TG):
                    pool.indirect_dma_start(out=buf[:, t, 0:D], out_offset=None, in_=rows_of,
                                            in_offset=bass.IndirectOffsetOnAxis(ap=at[:, t:t + 1], axis=0))\
                        .then_inc(done, COLS)

            for layer in range(4):
                if layer == 0:
                    pool.wait_ge(stored[0][0], COLS)
                else:
                    for b in range(2):
                        pool.wait_ge(stored[layer][b], COLS * STORES[layer] * (NBATCH // 2))
                with pool.If(spread == 0):
                    with pool.Fori(0, NG // 2) as i:
                        for b in range(2):
                            pool.wait_ge(idx_in[layer][b], (i + 1) * COLS)
                            pool.wait_ge(z_summed if layer == 3 else win_done[layer], 2 * i + b + 1)
                            pool.nop(nofuse=True)
                            gather(msg[:, b, :, :], table[layer], idx[:, b, :], gathered[layer][b])
                with pool.Else():
                    with pool.Fori(0, NG) as g:
                        pool.wait_ge(g_idx[layer], (g + 1) * COLS * (2 if layer == 3 else 1))
                        pool.wait_ge(g_free[layer], g + 1)
                        pool.nop(nofuse=True)
                        gather(msg[:, 0, :, :], table[layer], idx[:, 0, :], g_gathered[layer])
                        if layer == 3:
                            gather(q_rows[:, :, :], q_dram, didx[:, :], g_gathered[layer])

                def roots(j, b, i):
                    for k in range(ROOTS[layer]):
                        two = slice(0, 2 if layer == 0 and k == 0 else 1)
                        pool.wait_ge(asked[layer], j * ROOTS[layer] + k + 1)
                        pool.tensor_tensor(c3[:, two, :], c2[:, two, :], minus_half[:, 0:BB * two.stop]
                                           .rearrange("p (o k) -> p o k", k=BB), ALU.pow).then_inc(rooted[layer], 1)

                def split(j, b, i):
                    if layer != 2:
                        return
                    part = [q_s[b][:, :, p * D:(p + 1) * D] for p in range(3)]
                    pool.wait_ge(pq_read, j + 2)
                    pool.wait_ge(slot_stored[3], j + 1)
                    pool.nop(nofuse=True)
                    pool.tensor_copy(part[0], q_f[b][:, :, :]).then_inc(q_step, 1)
                    pool.wait_ge(q_step, 4 * j + 1)
                    pool.tensor_tensor(q_rest[:, :, :], q_f[b][:, :, :], part[0], ALU.subtract).then_inc(q_step, 1)
                    pool.wait_ge(q_step, 4 * j + 2)
                    pool.nop(nofuse=True)
                    pool.tensor_copy(part[1], q_rest[:, :, :]).then_inc(q_step, 1)
                    pool.wait_ge(q_step, 4 * j + 3)
                    pool.tensor_tensor(q_rest[:, :, :], q_rest[:, :, :], part[1], ALU.subtract).then_inc(q_step, 1)
                    pool.wait_ge(q_step, 4 * j + 4)
                    pool.nop(nofuse=True)
                    pool.tensor_copy(part[2], q_rest[:, :, :]).then_inc(q_split, 1)
                    pool.wait_ge(q_split, j + 1)

                skewed(pool, roots, split)
                if layer == 0:
                    pool.wait_ge(asked[0], NBATCH * ROOTS[0] + 1)
                    pool.tensor_tensor(dis_a[:, :], dis_a[:, :], minus_half[:, :], ALU.pow).then_inc(rooted[0], 1)
                if layer == 2:
                    pool.wait_ge(staged[2], NBATCH)
                    pool.memset(accT[0:D, :], 0.0).then_inc(cleared, 1)

        @block.tensor
        def _(pe):
            mm = nc.tensor.matmul
            for layer in range(4):
                pe.sem_inc(win_done[layer], 2)
                pe.sem_inc(products[layer], 2)
            for s, n in ((hist_mm, 2), (zed_done, 2), (g_zed, 1), (pq_done, 2), (y_done, 2)):
                pe.sem_inc(s, n)
            pe.wait_ge(consts, 6)
            pe.wait_ge(span_ready, 1)
            nc.tensor.transpose(pair[1][0:1, 0:P], span[:, 3:4], ident[:, :]).then_inc(span_turned, 1)
            mm(hist, zero16[:, :], zero16[:, 0:NB], start=True, stop=False)
            with pe.Fori(0, NG // 2) as i:
                for b in range(2):
                    pe.wait_ge(hist_oh, 2 * i + b + 1)
                    for t in range(TG):
                        last = mm(hist, hist_lo[:, b, t, :], hist_hi[:, b, t, :], start=False, stop=False)
                    last.then_inc(hist_mm, 1)
            mm(hist, zero16[:, :], zero16[:, 0:NB], start=False, stop=True).then_inc(hist_mm, 1)
            pe.wait_ge(ld_w, 4 * COLS)
            mm(pair[0][0:D + 1, 0:D], wt("w2t_b2"), wt("w3b"), start=True, stop=True).then_inc(w23_mm, 1)
            pe.wait_ge(w23_ready, 1)
            pe.wait_ge(cleared, 7)
            pe.wait_ge(flag_ready, 1)
            spread = pe.value_load(flag_i[0:1, 0:1], min_val=0, max_val=1)

            def scatter(layer, b, src):
                m = SUMS[layer]
                for t in range(TG):
                    last = mm(win[b][0:m, :], src[:, t, 0:m], onehot[:, b, t, :], start=t == 0, stop=t == TG - 1)
                return last

            def edge_products(b, stop):
                for h in range(2):
                    last = mm(zed[b][:, 4 * h:4 * h + 4, :].rearrange("p t d -> p (t d)"), edge_sb[:, b, h, :],
                              wt("edge", P), start=h == 0, stop=stop, skip_group_check=True)
                return last

            for layer in range(4):
                with pe.If(spread == 0):
                    with pe.Fori(0, NG // 2) as i:
                        for b in range(2):
                            g = 2 * i + b
                            if layer == 3:
                                pe.wait_ge(oh_ready[3], g + 1)
                                pe.wait_ge(turn_copied, g + 1)
                                pe.nop(nofuse=True)
                                for t in range(TG):
                                    last = nc.tensor.transpose(oh_t[b][:, t * P:(t + 1) * P],
                                                               onehot16[:, b, t, :], ident16[:, :])
                                last.then_inc(turn_done, 1)
                                pe.wait_ge(edge_in[b], (i + 1) * COLS)
                                pe.wait_ge(z_summed, g + 1)
                                edge_products(b, False)
                                pe.wait_ge(q_in[b], (i + 1) * COLS)
                                pe.wait_ge(turn_copied, g + 3)
                                for t in range(TG):
                                    for p in range(3):
                                        last = mm(zed[b][:, t, :], onehot_t[:, b, t * P:(t + 1) * P],
                                                  q_win[:, b, p * D:(p + 1) * D], start=False, stop=p == 2,
                                                  skip_group_check=True)
                                last.then_inc(zed_done, 1)
                                pe.wait_ge(silu_done, g + 1)
                            else:
                                pe.wait_ge(gathered[layer][b], (i + 1) * COLS * TG)
                                pe.wait_ge(oh_ready[layer], g + 1)
                            pe.wait_ge(acc_added[layer], g + 1)
                            scatter(layer, b, act_in[:, b, :, :] if layer == 3 else msg[:, b, :, :])\
                                .then_inc(win_done[layer], 1)
                with pe.Else():
                    with pe.Fori(0, NG) as g:
                        if layer == 3:
                            pe.wait_ge(g_edge, (g + 1) * COLS)
                            pe.wait_ge(g_sum, g + 1)
                            edge_products(0, True).then_inc(g_zed, 1)
                            pe.wait_ge(g_silu, g + 1)
                        else:
                            pe.wait_ge(g_gathered[layer], (g + 1) * COLS * TG)
                        pe.nop(nofuse=True)
                        with pe.Fori(0, NW) as w:
                            pe.wait_ge(g_oh[layer], g * NW + w + 1)
                            scatter(layer, 0, act_in[:, 0, :, :] if layer == 3 else msg[:, 0, :, :])\
                                .then_inc(g_win[layer], 1)

                def multiply(j, b, i):
                    pe.wait_ge(sx_ready if layer == 0 else staged[layer], j + 1)
                    for k in range(BB):
                        n = slice(k * P, (k + 1) * P)
                        to, ends = node_a[b][:, k, 0:D], k == BB - 1
                        if layer == 0:
                            mm(node_a[b][:, k, :], s_t[b][0:D + 2, n], wt("wn", D + 2), start=k == 0, stop=False,
                               skip_group_check=True)
                            mm(to, sx_t[b][0:D + 1, n], wt("wm", D + 1), start=False, stop=ends,
                               skip_group_check=True)
                            last = mm(node_b[b][:, k, :], x_tb[b][0:D + 1, n], wt("xn", D + 1), start=k == 0,
                                      stop=ends, skip_group_check=True)
                        elif layer == 3:
                            mm(to, s_t[b][0:D + 1, n], w23[:, :], start=k == 0, stop=False, skip_group_check=True)
                            last = mm(to, x_tb[b][0:D + 1, n], wt("w3a", D + 1), start=False, stop=ends,
                                      skip_group_check=True)
                        else:
                            last = mm(to, s_t[b][0:D, n], wt("w1" if layer == 1 else "w2"), start=k == 0,
                                      stop=ends, skip_group_check=True)
                    last.then_inc(products[layer], 1)

                def turn(j, b, i):
                    pe.wait_ge(u_done if layer == 3 else batch_done[layer], j + 1)
                    pe.wait_ge(turned_copied[layer], j + 1)
                    pe.nop(nofuse=True)
                    rows_in = (u if layer >= 2 else tab)[b]
                    for k in range(BB):
                        last = nc.tensor.transpose(node_t[0:D, k * P:(k + 1) * P], rows_in[:, k, :], ident[:, :])
                    last.then_inc(turned[layer], 1)
                    if layer == 2:
                        pe.wait_ge(turned_copied[2], j + 2)
                        pe.wait_ge(pq_read, j + 1)
                        for k in range(BB):
                            last = mm(node_pq[:, k * 2 * D:(k + 1) * 2 * D], x_tb[b][0:D + 1, k * P:(k + 1) * P],
                                      wt("pq", D + 1), start=k in (0, 4), stop=k in (3, BB - 1),
                                      skip_group_check=True)
                        last.then_inc(pq_done, 1)
                    if layer == 3:
                        pe.wait_ge(turned_copied[3], j + 2)
                        pe.wait_ge(batch_done[3], j + 1)
                        for k in range(BB):
                            last = mm(node_b[b][:, k, :], sx_t[b][0:D + 1, k * P:(k + 1) * P], wt("w4", D + 1),
                                      start=k == 0, stop=k == BB - 1, skip_group_check=True)
                        last.then_inc(y_done, 1)

                skewed(pe, multiply, turn)

        @block.scalar
        def _(act):
            copy = ACT.Copy
            for layer in range(4):
                act.sem_inc(turned_copied[layer], 1)
            act.sem_inc(turn_copied, 2)
            act.sem_inc(pq_read, 1)
            act.wait_ge(w23_mm, 1)
            nc.scalar.activation(w23[:, :], pair[0][0:D + 1, 0:D], copy).then_inc(w23_ready, 1)
            act.wait_ge(cleared, 7)
            act.wait_ge(ld_w, 4 * COLS)
            act.wait_ge(flag_ready, 1)
            spread = act.value_load(flag_i[0:1, 0:1], min_val=0, max_val=1)

            for layer in range(4):
                if layer == 3:
                    with act.If(spread == 0):
                        with act.Fori(0, NG // 2) as i:
                            for b in range(2):
                                g = 2 * i + b
                                act.wait_ge(turn_done, g + 1)
                                act.wait_ge(zed_done, g + 1)
                                nc.scalar.activation(onehot_t[:, b, :], oh_t[b], copy).then_inc(turn_copied, 1)
                                act.wait_ge(z_summed, g + 3)
                                nc.scalar.activation(act_in[:, b, :, :], act_in[:, b, :, :], ACT.Silu)\
                                    .then_inc(silu_done, 1)
                    with act.Else():
                        with act.Fori(0, NG) as g:
                            act.wait_ge(g_sum, g + 2)
                            nc.scalar.activation(act_in[:, 0, :, :], act_in[:, 0, :, :], ACT.Silu).then_inc(g_silu, 1)

                def stage(j, b, i):
                    act.wait_ge(products[layer], j + 1)
                    act.nop(nofuse=True)
                    if layer in (0, 3):
                        nc.scalar.activation(x_tb[b][0:D, :], XT[:, bass.ds(j * BN, BN)], copy)
                    nc.scalar.activation(s_t[b][0:READ[layer], :], accT[0:READ[layer], bass.ds(j * BN, BN)], copy)\
                        .then_inc(staged[layer], 1)

                def bring(j, b, i):
                    if layer == 3:
                        act.wait_ge(products[3], j + 3)
                        act.wait_ge(y_done, j + 1)
                        nc.scalar.activation(u[b][:, :, :], node_a[b][:, :, 0:D], ACT.Silu).then_inc(u_done, 1)
                    act.wait_ge(turned[layer], j + 1)
                    act.nop(nofuse=True)
                    if layer < 2:
                        nc.scalar.activation(accT[0:D, bass.ds(j * BN, BN)], node_t[0:D, 0:BN], copy)\
                            .then_inc(turned_copied[layer], 1)
                    elif layer == 2:
                        act.wait_ge(pq_done, j + 1)
                        act.nop(nofuse=True)
                        nc.scalar.activation(XT[:, bass.ds(j * BN, BN)], node_t[0:D, 0:BN], copy)
                        nc.scalar.activation(x_tb[b][0:D, :], node_t[0:D, 0:BN], copy).then_inc(turned_copied[2], 1)
                        act.wait_ge(pq_done, j + 3)
                        act.wait_ge(slot_stored[3], j + 1)
                        pq = node_pq[:, 0:BB * 2 * D].rearrange("p (k c) -> p k c", k=BB)
                        nc.scalar.activation(tab[b][:, :, :], pq[:, :, 0:D], copy)
                        nc.scalar.activation(q_f[b][:, :, :], pq[:, :, D:2 * D], copy).then_inc(pq_read, 1)
                    else:
                        nc.scalar.activation(sx_t[b][0:D, :], node_t[0:D, 0:BN], copy).then_inc(turned_copied[3], 1)

                act.wait_ge(pass_done[layer], 1)
                skewed(act, stage, bring)

        @block.vector
        def _(dve):
            v = nc.vector
            tt, ts, stt = v.tensor_tensor, v.tensor_scalar, v.scalar_tensor_tensor
            link = Chain(dve, dve_step)
            for layer in range(4):
                dve.sem_inc(acc_added[layer], 2)
                dve.sem_inc(g_free[layer], 1)
            dve.sem_inc(batch_done[3], 2)
            dve.sem_inc(z_summed, 2)
            dve.sem_inc(g_sum, 1)

            for b in range(2):
                v.memset(x_tb[b][D:D + 1, :], 1.0).then_inc(cleared, 1)
                v.memset(sx_t[b][D:D + 1, :], 1.0).then_inc(cleared, 1)
            dve.wait_ge(consts, 6)
            link(v.tensor_copy(iota_f[:, :], iota_i[:, :]))
            scratch = dst_rel[:, :].bitcast(I32)
            dve.wait_ge(ld_src, COLS)
            link(ts(scratch, edge_i[:, :], P - 1, None, ALU.bitwise_and))
            link(v.tensor_copy(src_lo[:, :], scratch))
            link(ts(scratch, edge_i[:, :], 7, None, ALU.logical_shift_right))
            v.tensor_copy(src_hi[:, :], scratch).then_inc(src_split, 1)
            dve.wait_ge(src_split, 1)
            dve.wait_ge(ld_first, 2 * COLS)
            link(v.tensor_copy(first_f[:, :], first_bc[:, :]))
            dve.wait_ge(ld_dst, COLS)
            link(v.tensor_copy(dst_f[:, :], edge_i[:, :]))
            link(tt(dst_rel[:, :].rearrange("p (g t) -> p g t", t=TG), dst_f[:, :].rearrange("p (g t) -> p g t", t=TG),
                    along(first_f[:, :], TG), ALU.subtract))
            link(v.tensor_reduce(span[:, 0:1], dst_rel[:, :], AX.X, ALU.max))
            link(v.tensor_reduce(span[:, 1:2], dst_rel[:, :], AX.X, ALU.min))
            link(ts(span[:, 2:3], span[:, 1:2], -1.0, None, ALU.mult))
            stt(span[:, 3:4], span[:, 0:1], float(1 - W), span[:, 2:3], ALU.add, ALU.max).then_inc(span_ready, 1)
            dve.wait_ge(span_turned, 1)
            link(v.tensor_reduce(flag_f[:, 0:1], pair[1][0:1, 0:P], AX.X, ALU.max))
            link(ts(flag_f[:, 1:2], flag_f[:, 0:1], 0.0, None, ALU.is_gt))
            v.tensor_copy(flag_i[:, :], flag_f[:, 1:2]).then_inc(flag_ready, 1)
            with dve.Fori(0, NG // 2) as i:
                for b in range(2):
                    g = 2 * i + b
                    dve.wait_ge(hist_mm, g + 1)
                    tt(hist_lo[:, b, :, :], iota_bc(P), along(cols(src_lo, g), P), ALU.is_equal)
                    tt(hist_hi[:, b, :, :], iota_bc(NB), along(cols(src_hi, g), NB), ALU.is_equal).then_inc(hist_oh, 1)
            dve.wait_ge(hist_mm, NG + 3)
            ts(r_out[:, :], hist, 1.0, None, ALU.max).then_inc(asked[-1], 1)
            dve.wait_ge(rooted[-1], 1)
            dve.wait_ge(ld_x, COLS)
            tt(X0[:, :, :], X[:, :, :], along(r_out[:, :], D), ALU.mult).then_inc(t0_ready, 1)
            dve.wait_ge(ld_w, 4 * COLS)
            dve.wait_ge(cleared, 7)
            dve.wait_ge(flag_ready, 1)
            link.close()
            spread = dve.value_load(flag_i[0:1, 0:1], min_val=0, max_val=1)

            def norm(to, x, eps, asks, gets, n, done=None):
                link(v.tensor_reduce(c1[:, :], x, AX.X, ALU.add))
                link(stt(t1[:, :, :], along(c1[:, :], D), -1.0 / D, x, ALU.mult, ALU.add))
                link(tt(t2[:, :, :], t1[:, :, :], t1[:, :, :], ALU.mult))
                link(v.tensor_reduce(c1[:, :], t2[:, :, :], AX.X, ALU.add))
                ts(c2[:, 0, :], c1[:, :], 1.0 / D, float(eps), ALU.mult, ALU.add).then_inc(asks, 1)
                dve.wait_ge(gets, n)
                last = tt(to, t1[:, :, :], along(c3[:, 0, :], D), ALU.mult)
                if done is None:
                    link(last)
                else:
                    last.then_inc(done, 1)

            for layer in range(4):
                m = SUMS[layer]
                if layer == 3:
                    for b in range(2):
                        v.memset(sx_t[b][D:D + 1, :], 1.0).then_inc(cleared, 1)
                    dve.wait_ge(cleared, 10)
                elif layer > 0:
                    dve.wait_ge(turned_copied[layer - 1], NBATCH + 1)
                with dve.If(spread == 0):
                    with dve.Fori(0, NG // 2) as i:
                        for b in range(2):
                            g = 2 * i + b
                            dve.wait_ge(win_done[layer], g + 1)
                            if layer == 2:
                                tt(onehot[:, b, :, :], iota_bc(W), along(cols(dst_rel, g), W), ALU.is_equal)\
                                    .then_inc(oh_raw, 1)
                                dve.wait_ge(oh_raw, g + 1)
                                tt(onehot[:, b, :, :], onehot[:, b, :, :], along(cols(weight_cols, g), W), ALU.mult)\
                                    .then_inc(oh_ready[2], 1)
                            elif layer == 0:
                                tt(onehot[:, b, :, :], iota_bc(W), along(cols(dst_rel, g), W), ALU.is_equal)
                                v.tensor_copy(msg[:, b, :, D + 1], cols(weight_cols, g)).then_inc(oh_ready[0], 1)
                            elif layer == 1:
                                tt(onehot[:, b, :, :], iota_bc(W), along(cols(dst_rel, g), W), ALU.is_equal)\
                                    .then_inc(oh_ready[1], 1)
                            else:
                                tt(onehot16[:, b, :, :], iota_bc(W), along(cols(dst_rel, g), W), ALU.is_equal)
                                tt(onehot[:, b, :, :], iota_bc(W), along(cols(dst_rel, g), W), ALU.is_equal)\
                                    .then_inc(oh_ready[3], 1)
                                dve.wait_ge(gathered[3][b], (i + 1) * COLS * TG)
                                dve.wait_ge(zed_done, g + 3)
                                tt(act_in[:, b, :, :], zed[b], msg[:, b, :, 0:D], ALU.add).then_inc(z_summed, 1)
                            first = dve.value_load(first_i[0:1, bass.ds(g, 1)], min_val=0, max_val=NP - W)
                            sums = accT[0:m, bass.ds(first, W)]
                            dve.wait_ge(win_done[layer], g + 3)
                            dve.wait_ge(acc_added[layer], g + 2)
                            tt(sums, sums, win[b][0:m, :], ALU.add).then_inc(acc_added[layer], 1)
                    dve.wait_ge(acc_added[layer], NG + 2)
                with dve.Else():
                    with dve.Fori(0, NG) as g:
                        if layer == 0:
                            v.tensor_copy(msg[:, 0, :, D + 1], cols(weight_cols, g))
                        if layer == 3:
                            dve.wait_ge(g_gathered[3], (g + 1) * COLS * 2 * TG)
                            dve.wait_ge(g_zed, g + 2)
                            tt(act_in[:, 0, :, :], zed[0], msg[:, 0, :, 0:D], ALU.add).then_inc(g_part, 1)
                            dve.wait_ge(g_part, g + 1)
                            tt(act_in[:, 0, :, :], act_in[:, 0, :, :], q_rows[:, :, :], ALU.add).then_inc(g_sum, 1)
                        v.tensor_copy(rel_w[:, :], cols(dst_f, g)).then_inc(g_rel[layer], 1)
                        with dve.Fori(0, NW) as w:
                            n = g * NW + w
                            dve.wait_ge(g_rel[layer], n + g + 1)
                            tt(onehot[:, 0, :, :], iota_bc(W), along(rel_w[:, :], W), ALU.is_equal)\
                                .then_inc(g_raw if layer == 2 else g_oh[layer], 1)
                            if layer == 2:
                                dve.wait_ge(g_raw, n + 1)
                                tt(onehot[:, 0, :, :], onehot[:, 0, :, :], along(cols(weight_cols, g), W), ALU.mult)\
                                    .then_inc(g_oh[2], 1)
                            sums = accT[0:m, bass.ds(w * W, W)]
                            dve.wait_ge(g_win[layer], n + 1)
                            ts(rel_w[:, :], rel_w[:, :], float(-W), None, ALU.add).then_inc(g_rel[layer], 1)
                            tt(sums, sums, win[0][0:m, :], ALU.add).then_inc(g_added[layer], 1)
                            dve.wait_ge(g_added[layer], n + 1)
                        dve.sem_inc(g_free[layer], 1)
                dve.sem_inc(pass_done[layer], 1)

                for_batch = {0: 8, 1: 16, 2: 8, 3: 13}[layer]
                with dve.Fori(0, NBATCH // 2) as i:
                    link.enter(i, 2 * for_batch)
                    for b in range(2):
                        j = 2 * i + b
                        blocks = bass.ds(j * BB, BB)
                        Xb, A = X[:, blocks, :], node_a[b][:, :, 0:D]
                        if layer == 0:
                            dve.wait_ge(staged[0], j + 1)
                            tt(sx_t[b][0:D + 1, :], s_t[b][0:D + 1, :], x_tb[b][0:D + 1, :], ALU.mult)\
                                .then_inc(sx_ready, 1)
                            dve.wait_ge(products[0], j + 3)
                            ts(c2[:, 0, :], node_a[b][:, :, D], 1.0, None, ALU.max)
                            ts(c2[:, 1, :], node_a[b][:, :, D], 1.0, None, ALU.add).then_inc(asked[0], 1)
                            v.tensor_copy(degrees[:, blocks, :], node_a[b][:, :, D:D + 2])
                            dve.wait_ge(rooted[0], 2 * j + 1)
                            tt(t1[:, :, :], A, along(c3[:, 0, :], D), ALU.mult)
                            link(v.tensor_copy(dinv1[:, blocks], c3[:, 1, :]))
                            link(tt(t1[:, :, :], t1[:, :, :], node_b[b], ALU.add))
                            link(tt(t2[:, :, :], t1[:, :, :], Xb, ALU.add))
                            norm(Xb, t2[:, :, :], 1e-5, asked[0], rooted[0], 2 * j + 2)
                            dve.wait_ge(slot_stored[1], j + 1)
                            tt(tab[b][:, :, :], Xb, along(dinv1[:, blocks], D), ALU.mult).then_inc(batch_done[0], 1)
                        elif layer == 1:
                            dve.wait_ge(products[1], j + 3)
                            link(tt(t1[:, :, :], A, along(dinv1[:, blocks], D), ALU.mult))
                            link(tt(t1[:, :, :], t1[:, :, :], row("b1"), ALU.add))
                            link(stt(t1[:, :, :], t1[:, :, :], 0.0, Xb, ALU.max, ALU.add))
                            norm(t2[:, :, :], t1[:, :, :], 1e-8, asked[1], rooted[1], 2 * j + 1)
                            link(tt(t2[:, :, :], t2[:, :, :], row("gamma1"), ALU.mult))
                            link(tt(t2[:, :, :], t2[:, :, :], row("beta1"), ALU.add))
                            link(tt(t2[:, :, :], t2[:, :, :], Xb, ALU.add))
                            norm(Xb, t2[:, :, :], 1e-5, asked[1], rooted[1], 2 * j + 2)
                            dve.wait_ge(slot_stored[2], j + 1)
                            tt(tab[b][:, :, :], Xb, along(dis2[:, blocks], D), ALU.mult).then_inc(batch_done[1], 1)
                        elif layer == 2:
                            dve.wait_ge(products[2], j + 3)
                            link(tt(t1[:, :, :], A, along(dis2[:, blocks], D), ALU.mult))
                            link(tt(t1[:, :, :], t1[:, :, :], row("b2"), ALU.add))
                            link(stt(t1[:, :, :], t1[:, :, :], 0.0, Xb, ALU.max, ALU.add))
                            norm(u[b][:, :, :], t1[:, :, :], 1e-5, asked[2], rooted[2], j + 1)
                            tt(Xb, t1[:, :, :], along(c3[:, 0, :], D), ALU.mult).then_inc(batch_done[2], 1)
                            dve.wait_ge(batch_done[2], j + 1)
                        else:
                            dve.wait_ge(y_done, j + 3)
                            link(tt(t1[:, :, :], node_b[b], Xb, ALU.add))
                            norm(t2[:, :, :], t1[:, :, :], 1e-5, asked[3], rooted[3], 2 * j + 1)
                            link(tt(t2[:, :, :], t2[:, :, :], row("gamma3"), ALU.mult))
                            link(tt(t2[:, :, :], t2[:, :, :], row("beta3"), ALU.add))
                            link(tt(t2[:, :, :], t2[:, :, :], Xb, ALU.add))
                            dve.wait_ge(slot_stored[4], j + 1)
                            norm(tab[b][:, :, :], t2[:, :, :], 1e-5, asked[3], rooted[3], 2 * j + 2, batch_done[3])
                            dve.wait_ge(batch_done[3], j + 3)
                link.leave(NBATCH // 2)
                if layer == 0:
                    link(ts(dis_a[:, :], degrees[:, :, 1], 1.0, None, ALU.add))
                    link(ts(dis_b[:, :], dis_a[:, :], 0.0, None, ALU.is_gt))
                    ts(dis_a[:, :], dis_a[:, :], TINY, None, ALU.max).then_inc(asked[0], 1)
                    dve.wait_ge(rooted[0], NBATCH * ROOTS[0] + 1)
                    link(tt(dis2[:, :], dis_a[:, :], dis_b[:, :], ALU.mult))
                    link.close()


def kernel(**inputs):
    import numpy as _np
    import concourse.bacc as _bacc
    from concourse import mybir as _mybir
    from concourse.bass_utils import run_bass_kernel_spmd as _run

    a = {name: _np.ascontiguousarray(x) for name, x in inputs.items()}
    n, e = a["x"].shape[0], a["src"].shape[0]
    n_pad, e_pad = shapes(n, e)
    NB, NG, f = n_pad // P, e_pad // GE, a["x"].dtype

    def edges(x, fill):
        full = _np.full((e_pad,), fill, x.dtype)
        full[:e] = x
        return _np.ascontiguousarray(full.reshape(NG, P, TG).transpose(1, 0, 2).reshape(P, NG * TG)), full

    src_cols, _ = edges(a["src"], n)
    dst_cols, dst_full = edges(a["dst"], n)
    w_cols, _ = edges(a["edge_weight"], 0)
    dst_first = _np.ascontiguousarray(_np.broadcast_to(dst_full[::GE], (P, NG)))
    x_full = _np.zeros((n_pad, D), f)
    x_full[:n] = a["x"]
    x_nodes = _np.ascontiguousarray(x_full.reshape(NB, P, D).transpose(1, 0, 2))
    x_t = _np.ascontiguousarray(x_full.T)
    edge_full = _np.zeros((e_pad, DE), f)
    edge_full[:e] = a["edge_attr_32"]
    edge_t = _np.ascontiguousarray(edge_full.reshape(NG, P, 2, 4, DE).transpose(3, 4, 0, 2, 1).reshape(P, NG * 2, P))

    weights = _np.zeros((P, WCOLS), f)

    def put(name, at_row, at_col, x):
        at = WEIGHTS[name][0] + at_col
        weights[at_row:at_row + x.shape[0], at:at + x.shape[1]] = x

    one = _np.ones((1, 1), f)
    w1, w3 = a["L3_gnn_w1"], a["L3_gnn_w3"]
    for k in range(4):
        put("edge", k * DE, k * D, w1[2 * D:])
    put("wn", 0, 0, a["L0_gnn_Wn"].T)
    put("wn", D, 0, a["L0_gnn_bn"][None])
    put("wn", D, D, one)
    put("wn", D + 1, D + 1, one)
    put("wm", 0, 0, a["L0_gnn_Wm"].T)
    put("wm", D, 0, a["L0_gnn_bm"][None])
    put("xn", 0, 0, a["L0_gnn_Wn"].T)
    put("xn", D, 0, a["L0_gnn_bn"][None])
    put("w1", 0, 0, a["L1_gnn_W"])
    put("w2", 0, 0, a["L2_gnn_W"].T)
    put("pq", 0, 0, w1[:D])
    put("pq", D, 0, a["L3_gnn_b1"][None])
    put("pq", 0, D, w1[D:2 * D])
    put("w2t_b2", 0, 0, a["L3_gnn_w2"].T)
    put("w2t_b2", 0, D, a["L3_gnn_b2"][:, None])
    put("w3b", 0, 0, w3[D:])
    put("w3a", 0, 0, w3[:D])
    put("w3a", D, 0, a["L3_gnn_b3"][None])
    put("w4", 0, 0, a["L3_gnn_w4"])
    put("w4", D, 0, a["L3_gnn_b4"][None])
    rows = _np.stack([a[k] for k in ("L1_gnn_b", "L1_gnn_ln_gamma", "L1_gnn_ln_beta", "L2_gnn_b", "L3_gnn_gamma",
                                     "L3_gnn_beta")])
    rows = _np.ascontiguousarray(_np.broadcast_to(rows, (P,) + rows.shape))

    nc = _bacc.Bacc("TRN2", target_bir_lowering=False, num_devices=1)
    arrays, args = {}, []
    for name, x in (("x_nodes", x_nodes), ("x_t", x_t), ("src_cols", src_cols), ("dst_cols", dst_cols),
                    ("dst_first", dst_first), ("w_cols", w_cols), ("edge_t", edge_t), ("weights", weights),
                    ("rows", rows)):
        arrays[f"in_{name}"] = x
        args.append(nc.dram_tensor(f"in_{name}", x.shape, _mybir.dt.from_np(x.dtype), kind="ExternalInput").ap())
    args.append(nc.dram_tensor("out_nodes", (P, NB, D), _mybir.dt.from_np(f), kind="ExternalOutput").ap())
    gnn_program(nc, *args)
    r = _run(nc, [arrays], core_ids=[0])
    return _np.ascontiguousarray(r.results[0]["out_nodes"].transpose(1, 0, 2).reshape(n_pad, D)[:n])
```

```python
from contextlib import ExitStack

import concourse.bass as bass
from concourse import mybir

F32 = mybir.dt.float32
BF16 = mybir.dt.bfloat16
I32 = mybir.dt.int32
ALU = mybir.AluOpType
ACT = mybir.ActivationFunctionType
AX = mybir.AxisListType

P = 128
D = 64
DE = 32
TG = 8
GE = P * TG
W = 38
WS = 16
HALF = TG // 2
BB = 5
COLS = 16
TINY = 1.1754944e-38


def padded(n, unit):
    return -(-n // unit) * unit


def shapes(n_nodes, n_edges):
    e_pad = padded(n_edges, 2 * GE)
    return padded(n_nodes + 1 + (e_pad - n_edges) * n_nodes // n_edges + W, 2 * BB * P), e_pad


WEIGHTS = {}
_at = 0
for _name, _cols in (("edge", 4 * D), ("wn", D + 2), ("wm", D), ("xn", D), ("w1", D), ("w2", D), ("pq", 2 * D),
                     ("w2t_b2", D + 1), ("w3b", D), ("w3a", D), ("w4", D)):
    WEIGHTS[_name] = (_at, _cols)
    _at += _cols
WCOLS = _at
ROWS = {name: k for k, name in enumerate(("b1", "gamma1", "beta1", "b2", "gamma3", "beta3"))}


class Chain:

    def __init__(self, engine, sem):
        self.engine, self.sem, self.done, self.base, self.n, self.per = engine, sem, 0, 0, 0, 0

    def enter(self, i, per):
        self.base, self.n, self.per = self.done + i * per, 0, per

    def leave(self, times):
        assert self.n == self.per, (self.n, self.per)
        self.done += times * self.per
        self.base, self.n = self.done, 0

    def __call__(self, ins):
        self.n += 1
        ins.then_inc(self.sem, 1)
        self.engine.wait_ge(self.sem, self.base + self.n)

    def close(self):
        self.done += self.n
        self.base, self.n = self.done, 0


def gnn_program(nc, x_nodes, x_t, src_cols, dst_cols, dst_first, w_cols, edge_t, weights, rows, out, n_nodes, n_edges):
    NB = x_nodes.shape[1]
    NP = NB * P
    NG = src_cols.shape[1] // TG
    NW = -(-NP // W)
    NBATCH = NB // BB
    BN = BB * P
    PAIRS = NG // 2
    NH = n_nodes // P + 1
    HI = [(NH * q // 4, NH * (q + 1) // 4) for q in range(4)]
    assert all((h1 - h0) * W <= 512 for h0, h1 in HI)

    SHARE = [min(max(round((t + 0.5) * P * n_nodes / n_edges - WS / 2), 0), W - WS) for t in range(TG)]
    SHARE[0], SHARE[-1] = 0, W - WS
    if any(b - a > WS for a, b in zip(SHARE, SHARE[1:])):
        SHARE = [t * (W - WS) // (TG - 1) for t in range(TG)]

    ctx = ExitStack()
    with ctx:
        def sb(name, shape, dt=F32):
            return ctx.enter_context(nc.sbuf_tensor(name, shape, dt))

        def ps(name, shape, dt=F32):
            return ctx.enter_context(nc.psum_tensor(name, shape, dt))

        def sem(name):
            return ctx.enter_context(nc.semaphore(name))

        table = [nc.dram_tensor(f"table{n}", (NP, D), F32, kind="Internal").ap() for n in range(4)]
        q_parts_dram = nc.dram_tensor("q_parts_dram", (NP, 3 * D), BF16, kind="Internal").ap()
        q_dram = nc.dram_tensor("q_dram", (NP, D), F32, kind="Internal").ap()

        X = sb("X", [P, NB, D])
        XT = sb("XT", [D, NP])
        accT = sb("accT", [D + 2, NW * W])
        weight_cols = sb("weight_cols", [P, NG * TG])
        edge_i = sb("edge_i", [P, NG * TG], I32)
        dst_rel = sb("dst_rel", [P, NG * TG])
        src_lo = sb("src_lo", [P, NG * TG], BF16)
        src_hi = sb("src_hi", [P, NG * TG], BF16)
        xparts = sb("xparts", [P, NB, 3 * D], BF16)
        first_i = sb("first_i", [1, NG], I32)
        first_bc = sb("first_bc", [P, NG], I32)
        first_f = sb("first_f", [P, NG])
        Wt = sb("Wt", [P, WCOLS])
        R = sb("R", [P, len(ROWS), D])
        w23 = sb("w23", [D + 1, D])
        ident = sb("ident", [P, P])
        ident16 = sb("ident16", [P, P], BF16)
        iota_z = sb("iota_z", [P, NH * WS], mybir.dt.float16)
        iota_f = sb("iota_f", [P, P])
        zero16 = sb("zero16", [P, P], BF16)
        degrees = sb("degrees", [P, NB, 2])
        r_out = sb("r_out", [P, NB])
        dinv1 = sb("dinv1", [P, NB])
        dis2 = sb("dis2", [P, NB])
        dis_a = sb("dis_a", [P, NB])
        dis_b = sb("dis_b", [P, NB])
        span = sb("span", [P, 5])
        flag_i = sb("flag_i", [1, 1], I32)
        flag_f = sb("flag_f", [1, 2])

        idx = sb("idx", [P, 2, TG], I32)
        didx = sb("didx", [P, TG], I32)
        msg = sb("msg", [P, 2, TG, D + 2])
        act_in = sb("act_in", [P, 2, TG, D])
        q_rows = act_in[:, 1, :, :]
        edge_sb = sb("edge_sb", [P, 2, 2, P])
        q_win = sb("q_win", [W, 2, 3 * D], BF16)
        onehot = sb("onehot", [P, 2, TG, W])
        onehot16 = sb("onehot16", [P, 2, TG, W], BF16)
        onehot_t = sb("onehot_t", [W, 2, GE], BF16)
        hist_lo = sb("hist_lo", [P, 2, TG, P], BF16)
        hist_hi = sb("hist_hi", [P, 2, TG, NB], BF16)
        zrows = sb("zrows", [P, TG, NB * WS], BF16)
        X0 = zrows[:, :, :].rearrange("p t c -> p (t c)").bitcast(F32)[:, 0:NB * D].rearrange("p (k d) -> p k d", d=D)
        comb = edge_i[:, :].bitcast(F32)
        counts = sb("counts", [P, 2, NH * W], BF16)
        ones_w = sb("ones_w", [P, 2, TG, D + 2])
        onehot_c = sb("onehot_c", [P, 2, TG, W])
        rel_w = sb("rel_w", [P, TG])

        s_t = [sb(f"s_t{b}", [D + 2, BN]) for b in range(2)]
        x_tb = [sb(f"x_tb{b}", [D + 1, BN]) for b in range(2)]
        sx_t = [sb(f"sx_t{b}", [D + 1, BN]) for b in range(2)]
        u = [sb(f"u{b}", [P, BB, D]) for b in range(2)]
        tab = [sb(f"tab{b}", [P, BB, D]) for b in range(2)]
        q_f = [sb(f"q_f{b}", [P, BB, D]) for b in range(2)]
        q_s = [xparts[:, b * BB:(b + 1) * BB, :] for b in range(2)]
        q_rest = sb("q_rest", [P, BB, D])
        t1 = sb("t1", [P, BB, D])
        t2 = sb("t2", [P, BB, D])
        c1 = sb("c1", [P, BB])
        c2 = sb("c2", [P, 2, BB])
        c3 = sb("c3", [P, 2, BB])
        minus_half = sb("minus_half", [P, NB])

        bank = [ps(f"bank{n}", [P, 512]) for n in range(4)]
        pair = [ps(f"pair{n}", [P, 1024]) for n in range(2)]
        win = [bank[b][:, 0:W] for b in range(2)]
        cwin_ab = [bank[2 + b][:, 0:W] for b in range(2)]
        cwin_c = [bank[2 + b][:, 64:64 + W] for b in range(2)]
        count_banks = [pair[q // 2][:, 512 * (q % 2):512 * (q % 2) + (HI[q][1] - HI[q][0]) * W] for q in range(4)]
        zed = [bank[2 + b][:, :].rearrange("p (t d) -> p t d", t=TG) for b in range(2)]
        oh_t = [pair[b][0:W, 0:512].bitcast(BF16) for b in range(2)]
        node_a = [bank[2 + b][:, 0:BB * (D + 2)].rearrange("p (k d) -> p k d", k=BB) for b in range(2)]
        node_b = [pair[0][:, 512 * b:512 * b + BB * D].rearrange("p (k d) -> p k d", k=BB) for b in range(2)]
        node_pq = pair[0]
        node_t = pair[1]
        hist = bank[0][:, 0:NB]

        ld_x, ld_src, ld_dst, ld_first, ld_w = (sem(n) for n in ("ld_x", "ld_src", "ld_dst", "ld_first", "ld_w"))
        consts, dve_step, src_split = sem("consts"), sem("dve_step"), sem("src_split")
        hist_oh, hist_mm = sem("hist_oh"), sem("hist_mm")
        span_ready, span_turned, flag_ready = sem("span_ready"), sem("span_turned"), sem("flag_ready")
        w23_mm, w23_ready, t0_ready, cleared = sem("w23_mm"), sem("w23_ready"), sem("t0_ready"), sem("cleared")

        def per_layer(name, layers=range(4)):
            return {n: sem(f"{name}_{n}") for n in layers}

        def per_slot(name, layers=range(4)):
            return {n: [sem(f"{name}_{n}{b}") for b in range(2)] for n in layers}

        idx_in = {n: [sem(f"idx_in_{n}{b}") for b in range(2)] for n in range(4)}
        gathered = {n: [sem(f"gathered_{n}{b}") for b in range(2)] for n in range(4)}
        z_ready, z_used, counted = (per_layer(n, (0, 1)) for n in ("z_ready", "z_used", "counted"))
        cwin_done, c_part, c_added = (per_layer(n, (0, 1)) for n in ("cwin_done", "c_part", "c_added"))
        parts_ready = sem("parts_ready")
        oh_raw = sem("oh_raw")
        oh_ready, win_done, acc_added = per_layer("oh_ready"), per_layer("win_done"), per_layer("acc_added")
        edge_in, q_in = [sem(f"edge_in{b}") for b in range(2)], [sem(f"q_in{b}") for b in range(2)]
        turn_done, turn_copied, zed_done = sem("turn_done"), sem("turn_copied"), sem("zed_done")
        z_summed, silu_done = sem("z_summed"), sem("silu_done")
        g_idx, g_gathered, g_free = per_layer("g_idx"), per_layer("g_gathered"), per_layer("g_free")
        g_rel, g_raw, g_oh = per_layer("g_rel"), sem("g_raw"), per_layer("g_oh")
        g_win, g_added = per_layer("g_win"), per_layer("g_added")
        g_edge, g_zed, g_part, g_sum, g_silu = (sem(n) for n in ("g_edge", "g_zed", "g_part", "g_sum", "g_silu"))
        pass_done = sem("pass_done")
        asked, rooted = sem("asked"), sem("rooted")
        staged, products, batch_done = per_layer("staged"), per_layer("products"), per_layer("batch_done")
        turned, turned_copied = per_layer("turned"), per_layer("turned_copied")
        sx_ready, pq_done, pq_read = (sem(n) for n in ("sx_ready", "pq_done", "pq_read"))
        split_done, split_step = per_layer("split_done", (0, 2)), per_layer("split_step", (0, 2))
        u_done, y_done = sem("u_done"), sem("y_done")
        stored = per_slot("stored")
        stored[4] = [sem(f"stored_4{b}") for b in range(2)]

        slot_stored = per_layer("slot_stored", (1, 2, 3, 4))

        STORES = {1: 1, 2: 1, 3: 3, 4: 1}

        def wt(name, k=D):
            at, cols = WEIGHTS[name]
            return Wt[0:k, at:at + cols]

        def row(name, n=BB):
            return R[:, ROWS[name], :].rearrange("p (k d) -> p k d", k=1).broadcast_to((P, n, D))

        def cols(t, g, n=TG):
            return t[:, bass.ds(g * TG, n)]

        def along(ap, n):
            return ap.rearrange("p (k o) -> p k o", o=1).broadcast_to((P, ap.shape[1], n))

        def iota_bc(n, k=TG):
            return iota_f[:, 0:n].rearrange("p (k n) -> p k n", k=1).broadcast_to((P, k, n))

        SUMS = {0: D + 2, 1: D, 2: D, 3: D}
        READ = {0: D + 2, 1: D, 2: D, 3: D + 1}
        ROOTS = {0: 2, 1: 2, 2: 1, 3: 2}
        ROOTS_BEFORE = {0: 1}
        for layer in (1, 2, 3):
            ROOTS_BEFORE[layer] = ROOTS_BEFORE[layer - 1] + ROOTS[layer - 1] * NBATCH + (layer == 1)

        def gathered_groups(eng, layer):
            n = PAIRS if layer < 2 else NG
            with eng.Fori(0, n // 2) as i:
                yield i, (0, 1)
            if n % 2:
                yield n // 2, (0,)

        def two_by_two(eng, layer):
            if layer >= 2:
                with eng.Fori(0, NG // 2) as i:
                    yield i

        def group(layer, n):
            return 2 * n if layer < 2 else n

        def skewed_pairs(eng, first, second):
            first(0, 0, 0)
            with eng.Fori(0, (PAIRS - 1) // 2) as i:
                first(2 * i + 1, 1, i)
                second(2 * i, 0, i)
                first(2 * i + 2, 0, i + 1)
                second(2 * i + 1, 1, i)
            if PAIRS % 2 == 0:
                first(PAIRS - 1, 1, PAIRS // 2 - 1)
                second(PAIRS - 2, 0, PAIRS // 2 - 1)
            second(PAIRS - 1, (PAIRS - 1) % 2, (PAIRS - 1) // 2)

        def skewed(eng, first, second):
            first(0, 0, 0)
            with eng.Fori(0, NBATCH // 2 - 1) as i:
                first(2 * i + 1, 1, i)
                second(2 * i, 0, i)
                first(2 * i + 2, 0, i + 1)
                second(2 * i + 1, 1, i)
            first(NBATCH - 1, 1, NBATCH // 2 - 1)
            second(NBATCH - 2, 0, NBATCH // 2 - 1)
            second(NBATCH - 1, 1, NBATCH // 2 - 1)

        block = ctx.enter_context(nc.Block())

        @block.sync
        def _(sp):
            sp.dma_start(edge_i[:, :], src_cols).then_inc(ld_src, COLS)
            sp.dma_start(first_i[:, :], dst_first[0:1, :]).then_inc(ld_first, COLS)
            sp.dma_start(first_bc[:, :], dst_first).then_inc(ld_first, COLS)
            sp.dma_start(X[:, :, :], x_nodes).then_inc(ld_x, COLS)
            sp.wait_ge(src_split, 1)
            sp.dma_start(edge_i[:, :], dst_cols).then_inc(ld_dst, COLS)
            sp.dma_start(Wt[:, :], weights).then_inc(ld_w, COLS)
            sp.dma_start(R[:, :, :], rows).then_inc(ld_w, COLS)
            sp.dma_start(weight_cols[:, :], w_cols).then_inc(ld_w, COLS)
            sp.dma_start(XT[:, :], x_t).then_inc(ld_w, COLS)
            for n in (1, 2, 3, 4):
                sp.sem_inc(slot_stored[n], 2)
            sp.wait_ge(t0_ready, 1)
            sp.dma_start(table[0].rearrange("(k p) d -> p k d", p=P), X0).then_inc(stored[0][0], COLS)
            sp.wait_ge(flag_ready, 1)
            spread = sp.value_load(flag_i[0:1, 0:1], min_val=0, max_val=1)

            for layer in range(4):
                if layer == 3:
                    for b in range(2):
                        sp.wait_ge(stored[3][b], COLS * STORES[3] * (NBATCH // 2))
                with sp.If(spread == 0):
                    for i, slots in gathered_groups(sp, layer):
                        for b in slots:
                            n = 2 * i + b
                            g = group(layer, n)
                            sp.wait_ge(z_summed if layer == 3 else win_done[layer], n + 1)
                            sp.dma_start(idx[:, b, :], cols(src_cols, g)).then_inc(idx_in[layer][b], COLS)
                            if layer == 3:
                                first = sp.value_load(first_i[0:1, bass.ds(g, 1)], min_val=0, max_val=NP - W)
                                sp.wait_ge(zed_done, g + 1)
                                sp.dma_start(edge_sb[:, b, :, :], edge_t[:, bass.ds(g * 2, 2), :])\
                                  .then_inc(edge_in[b], COLS)
                                sp.dma_start(q_win[:, b, :], q_parts_dram[bass.ds(first, W), :])\
                                  .then_inc(q_in[b], COLS)
                with sp.Else():
                    with sp.Fori(0, NG) as g:
                        sp.wait_ge(g_free[layer], g + 1)
                        sp.dma_start(idx[:, 0, :], cols(src_cols, g)).then_inc(g_idx[layer], COLS)
                        if layer == 3:
                            sp.dma_start(didx[:, :], cols(dst_cols, g)).then_inc(g_idx[layer], COLS)
                            sp.wait_ge(g_zed, g + 1)
                            sp.dma_start(edge_sb[:, 0, :, :], edge_t[:, bass.ds(g * 2, 2), :]).then_inc(g_edge, COLS)

                with sp.Fori(0, NBATCH // 2) as i:
                    for b in range(2):
                        j = 2 * i + b
                        of_batch = bass.ds(j * BN, BN)
                        if layer < 2:
                            sp.wait_ge(batch_done[layer], j + 1)
                            sp.dma_start(table[layer + 1][of_batch, :].rearrange("(k p) d -> p k d", p=P),
                                         tab[b][:, :, :]).then_inc(stored[layer + 1][b], COLS)
                        elif layer == 2:
                            sp.wait_ge(pq_read, j + 2)
                            sp.dma_start(table[3][of_batch, :].rearrange("(k p) d -> p k d", p=P),
                                         tab[b][:, :, :]).then_inc(stored[3][b], COLS)
                            sp.dma_start(q_dram[of_batch, :].rearrange("(k p) d -> p k d", p=P),
                                         q_f[b][:, :, :]).then_inc(stored[3][b], COLS)
                            sp.wait_ge(split_done[2], j + 1)
                            sp.dma_start(q_parts_dram[of_batch, :].rearrange("(k p) d -> p k d", p=P),
                                         q_s[b]).then_inc(stored[3][b], COLS)
                        else:
                            sp.wait_ge(batch_done[3], j + 3)
                            sp.dma_start(out[:, bass.ds(j * BB, BB), :], tab[b][:, :, :]).then_inc(stored[4][b], COLS)
                        sp.wait_ge(stored[layer + 1][b], COLS * STORES[layer + 1] * (i + 1))
                        sp.sem_inc(slot_stored[layer + 1], 1)
            for b in range(2):
                sp.wait_ge(stored[4][b], COLS * (NBATCH // 2))

        @block.gpsimd
        def _(pool):
            pool.memset(ident[:, :], 0.0).then_inc(consts, 1)
            pool.memset(ident16[:, :], 0.0).then_inc(consts, 1)
            pool.iota(iota_f[:, :], pattern=[[1, P]], base=0, channel_multiplier=0,
                      allow_small_or_imprecise_dtypes=True).then_inc(consts, 1)
            pool.iota(iota_z[:, :], pattern=[[1, NH * WS]], base=0, channel_multiplier=0,
                      allow_small_or_imprecise_dtypes=True).then_inc(consts, 1)
            pool.memset(ones_w[:, :, :, 0:D], 0.0).then_inc(consts, 1)
            pool.memset(ones_w[:, :, :, D:D + 2], 1.0).then_inc(consts, 1)
            pool.memset(zero16[:, :], 0.0).then_inc(consts, 1)
            pool.wait_ge(consts, 7)
            for m in (ident, ident16):
                pool.affine_select(out=m[:, :], in_=m[:, :], compare_op=ALU.not_equal, fill=1.0, base=0,
                                   pattern=[[-1, P]], channel_multiplier=1).then_inc(consts, 1)
            pool.memset(minus_half[:, :], -0.5).then_inc(cleared, 1)
            pool.memset(msg[:, :, :, :], 1.0).then_inc(cleared, 1)
            pool.memset(accT[:, :], 0.0).then_inc(cleared, 1)
            pool.wait_ge(cleared, 7)
            pool.sem_inc(split_done[0], 2)
            pool.wait_ge(asked, 1)
            pool.tensor_tensor(r_out[:, :], r_out[:, :], minus_half[:, :], ALU.pow).then_inc(rooted, 1)
            pool.wait_ge(flag_ready, 1)
            spread = pool.value_load(flag_i[0:1, 0:1], min_val=0, max_val=1)

            def gather(buf, rows_of, at, done):
                for t in range(TG):
                    pool.indirect_dma_start(out=buf[:, t, 0:D], out_offset=None, in_=rows_of,
                                            in_offset=bass.IndirectOffsetOnAxis(ap=at[:, t:t + 1], axis=0))\
                        .then_inc(done, COLS)

            for layer in range(4):
                if layer == 0:
                    pool.wait_ge(stored[0][0], COLS)
                else:
                    for b in range(2):
                        pool.wait_ge(stored[layer][b], COLS * STORES[layer] * (NBATCH // 2))
                with pool.If(spread == 0):
                    for i, slots in gathered_groups(pool, layer):
                        for b in slots:
                            pool.wait_ge(idx_in[layer][b], (i + 1) * COLS)
                            pool.wait_ge(z_summed if layer == 3 else win_done[layer], 2 * i + b + 1)
                            pool.nop(nofuse=True)
                            gather(msg[:, b, :, :], table[layer], idx[:, b, :], gathered[layer][b])
                with pool.Else():
                    with pool.Fori(0, NG) as g:
                        pool.wait_ge(g_idx[layer], (g + 1) * COLS * (2 if layer == 3 else 1))
                        pool.wait_ge(g_free[layer], g + 1)
                        pool.nop(nofuse=True)
                        gather(msg[:, 0, :, :], table[layer], idx[:, 0, :], g_gathered[layer])
                        if layer == 3:
                            gather(q_rows[:, :, :], q_dram, didx[:, :], g_gathered[layer])

                def roots(j, b, i):
                    for k in range(ROOTS[layer]):
                        two = slice(0, 2 if layer == 0 and k == 0 else 1)
                        pool.wait_ge(asked, ROOTS_BEFORE[layer] + j * ROOTS[layer] + k + 1)
                        pool.tensor_tensor(c3[:, two, :], c2[:, two, :], minus_half[:, 0:BB * two.stop]
                                           .rearrange("p (o k) -> p o k", k=BB), ALU.pow).then_inc(rooted, 1)

                def split(j, b, i):
                    if layer not in (0, 2):
                        return
                    if layer == 0:
                        rows_in, parts = tab[b], xparts[:, bass.ds(j * BB, BB), :]
                        pool.wait_ge(batch_done[0], j + 1)
                    else:
                        rows_in, parts = q_f[b], q_s[b]
                        pool.wait_ge(pq_read, j + 2)
                        pool.wait_ge(slot_stored[3], j + 1)
                    step = split_step[layer]
                    pool.nop(nofuse=True)
                    pool.tensor_copy(parts[:, :, 0:D], rows_in[:, :, :]).then_inc(step, 1)
                    pool.wait_ge(step, 4 * j + 1)
                    pool.nop(nofuse=True)
                    pool.tensor_tensor(q_rest[:, :, :], rows_in[:, :, :], parts[:, :, 0:D], ALU.subtract)\
                        .then_inc(step, 1)
                    pool.wait_ge(step, 4 * j + 2)
                    pool.nop(nofuse=True)
                    pool.tensor_copy(parts[:, :, D:2 * D], q_rest[:, :, :]).then_inc(step, 1)
                    pool.wait_ge(step, 4 * j + 3)
                    pool.nop(nofuse=True)
                    pool.tensor_tensor(q_rest[:, :, :], q_rest[:, :, :], parts[:, :, D:2 * D], ALU.subtract)\
                        .then_inc(step, 1)
                    pool.wait_ge(step, 4 * j + 4)
                    pool.nop(nofuse=True)
                    pool.tensor_copy(parts[:, :, 2 * D:3 * D], q_rest[:, :, :]).then_inc(split_done[layer], 1)
                    pool.wait_ge(split_done[layer], j + (3 if layer == 0 else 1))

                skewed(pool, roots, split)
                if layer == 0:
                    pool.wait_ge(asked, ROOTS_BEFORE[1])
                    pool.tensor_tensor(dis_a[:, :], dis_a[:, :], minus_half[:, :], ALU.pow).then_inc(rooted, 1)
                if layer == 2:
                    pool.wait_ge(staged[2], NBATCH)
                    pool.memset(accT[0:D, :], 0.0).then_inc(cleared, 1)

        @block.tensor
        def _(pe):
            mm = nc.tensor.matmul
            for layer in range(4):
                pe.sem_inc(win_done[layer], 2)
                if layer < 2:
                    pe.sem_inc(z_used[layer], 2)
                    pe.sem_inc(cwin_done[layer], 2)
                pe.sem_inc(products[layer], 2)
            for s, n in ((hist_mm, 2), (zed_done, 2), (g_zed, 1), (pq_done, 2), (y_done, 2)):
                pe.sem_inc(s, n)
            pe.wait_ge(consts, 9)
            pe.wait_ge(span_ready, 1)
            nc.tensor.transpose(pair[1][0:1, 0:P], span[:, 4:5], ident[:, :]).then_inc(span_turned, 1)
            mm(hist, zero16[:, :], zero16[:, 0:NB], start=True, stop=False)
            with pe.Fori(0, NG // 2) as i:
                for b in range(2):
                    pe.wait_ge(hist_oh, 2 * i + b + 1)
                    for t in range(TG):
                        last = mm(hist, hist_lo[:, b, t, :], hist_hi[:, b, t, :], start=False, stop=False)
                    last.then_inc(hist_mm, 1)
            mm(hist, zero16[:, :], zero16[:, 0:NB], start=False, stop=True).then_inc(hist_mm, 1)
            pe.wait_ge(ld_w, 4 * COLS)
            mm(pair[0][0:D + 1, 0:D], wt("w2t_b2"), wt("w3b"), start=True, stop=True).then_inc(w23_mm, 1)
            pe.wait_ge(w23_ready, 1)
            pe.wait_ge(cleared, 7)
            pe.wait_ge(flag_ready, 1)
            spread = pe.value_load(flag_i[0:1, 0:1], min_val=0, max_val=1)

            def scatter(layer, b, src):
                m = SUMS[layer]
                for t in range(TG):
                    last = mm(win[b][0:m, :], src[:, t, 0:m], onehot[:, b, t, :], start=t == 0, stop=t == TG - 1)
                return last

            def edge_products(b, stop):
                for h in range(2):
                    last = mm(zed[b][:, 4 * h:4 * h + 4, :].rearrange("p t d -> p (t d)"), edge_sb[:, b, h, :],
                              wt("edge", P), start=h == 0, stop=stop, skip_group_check=True)
                return last

            for layer in range(4):
                with pe.If(spread == 0):
                    def count(n, b, i):
                        pe.wait_ge(counted[layer], n + 1)
                        for t in range(TG):
                            if t % HALF == 0:
                                pe.wait_ge(z_ready[layer], 2 * n + t // HALF + 1)
                            for q in range(4):
                                to = count_banks[q].rearrange("p (h w) -> p h w", w=W)[:, :, SHARE[t]:SHARE[t] + WS]
                                last = mm(to, hist_lo[:, b, t, :], zrows[:, t, HI[q][0] * WS:HI[q][1] * WS],
                                          start=t == 0, stop=t == TG - 1, skip_group_check=True)
                            if t % HALF == HALF - 1:
                                last.then_inc(z_used[layer], 1)

                    def sum_pair(n, b, i):
                        pe.wait_ge(gathered[layer][b], (i + 1) * COLS * TG)
                        pe.wait_ge(oh_ready[layer], n + 1)
                        pe.wait_ge(acc_added[layer], n + 1)
                        scatter(layer, b, msg[:, b, :, :]).then_inc(win_done[layer], 1)
                        if layer == 0:
                            pe.wait_ge(parts_ready, 1)
                        else:
                            pe.wait_ge(split_done[0], NBATCH + 2)
                        pe.wait_ge(counted[layer], n + 2)
                        pe.wait_ge(c_added[layer], n + 1)
                        for h in range(NH):
                            of_h = counts[:, b, h * W:(h + 1) * W]
                            mm(cwin_ab[b], xparts[:, h, 0:2 * D], of_h, start=h == 0, stop=h == NH - 1,
                               skip_group_check=True)
                            last = mm(cwin_c[b][0:D, :], xparts[:, h, 2 * D:3 * D], of_h, start=False,
                                      stop=h == NH - 1, skip_group_check=True)
                        if layer == 0:
                            for t in range(TG):
                                last = mm(cwin_c[b][0:D + 2, :], ones_w[:, b, t, :], onehot_c[:, b, t, :],
                                          start=False, stop=t == TG - 1, skip_group_check=True)
                        last.then_inc(cwin_done[layer], 1)

                    if layer < 2:
                        skewed_pairs(pe, count, sum_pair)
                    for i in two_by_two(pe, layer):
                        for b in range(2):
                            g = 2 * i + b
                            if layer == 3:
                                pe.wait_ge(oh_ready[3], g + 1)
                                pe.wait_ge(turn_copied, g + 1)
                                pe.nop(nofuse=True)
                                for t in range(TG):
                                    last = nc.tensor.transpose(oh_t[b][:, t * P:(t + 1) * P],
                                                               onehot16[:, b, t, :], ident16[:, :])
                                last.then_inc(turn_done, 1)
                                pe.wait_ge(edge_in[b], (i + 1) * COLS)
                                pe.wait_ge(z_summed, g + 1)
                                edge_products(b, False)
                                pe.wait_ge(q_in[b], (i + 1) * COLS)
                                pe.wait_ge(turn_copied, g + 3)
                                for t in range(TG):
                                    for p in range(3):
                                        last = mm(zed[b][:, t, :], onehot_t[:, b, t * P:(t + 1) * P],
                                                  q_win[:, b, p * D:(p + 1) * D], start=False, stop=p == 2,
                                                  skip_group_check=True)
                                last.then_inc(zed_done, 1)
                                pe.wait_ge(silu_done, g + 1)
                            else:
                                pe.wait_ge(gathered[layer][b], (i + 1) * COLS * TG)
                                pe.wait_ge(oh_ready[layer], g + 1)
                            pe.wait_ge(acc_added[layer], g + 1)
                            scatter(layer, b, act_in[:, b, :, :] if layer == 3 else msg[:, b, :, :])\
                                .then_inc(win_done[layer], 1)
                with pe.Else():
                    with pe.Fori(0, NG) as g:
                        if layer == 3:
                            pe.wait_ge(g_edge, (g + 1) * COLS)
                            pe.wait_ge(g_sum, g + 1)
                            edge_products(0, True).then_inc(g_zed, 1)
                            pe.wait_ge(g_silu, g + 1)
                        else:
                            pe.wait_ge(g_gathered[layer], (g + 1) * COLS * TG)
                        pe.nop(nofuse=True)
                        with pe.Fori(0, NW) as w:
                            pe.wait_ge(g_oh[layer], g * NW + w + 1)
                            scatter(layer, 0, act_in[:, 0, :, :] if layer == 3 else msg[:, 0, :, :])\
                                .then_inc(g_win[layer], 1)

                def multiply(j, b, i):
                    pe.wait_ge(sx_ready if layer == 0 else staged[layer], j + 1)
                    for k in range(BB):
                        n = slice(k * P, (k + 1) * P)
                        to, ends = node_a[b][:, k, 0:D], k == BB - 1
                        if layer == 0:
                            mm(node_a[b][:, k, :], s_t[b][0:D + 2, n], wt("wn", D + 2), start=k == 0, stop=False,
                               skip_group_check=True)
                            mm(to, sx_t[b][0:D + 1, n], wt("wm", D + 1), start=False, stop=ends,
                               skip_group_check=True)
                            last = mm(node_b[b][:, k, :], x_tb[b][0:D + 1, n], wt("xn", D + 1), start=k == 0,
                                      stop=ends, skip_group_check=True)
                        elif layer == 3:
                            mm(to, s_t[b][0:D + 1, n], w23[:, :], start=k == 0, stop=False, skip_group_check=True)
                            last = mm(to, x_tb[b][0:D + 1, n], wt("w3a", D + 1), start=False, stop=ends,
                                      skip_group_check=True)
                        else:
                            last = mm(to, s_t[b][0:D, n], wt("w1" if layer == 1 else "w2"), start=k == 0,
                                      stop=ends, skip_group_check=True)
                    last.then_inc(products[layer], 1)

                def turn(j, b, i):
                    pe.wait_ge(u_done if layer == 3 else batch_done[layer], j + 1)
                    pe.wait_ge(turned_copied[layer], j + 1)
                    pe.nop(nofuse=True)
                    rows_in = (u if layer >= 2 else tab)[b]
                    for k in range(BB):
                        last = nc.tensor.transpose(node_t[0:D, k * P:(k + 1) * P], rows_in[:, k, :], ident[:, :])
                    last.then_inc(turned[layer], 1)
                    if layer == 2:
                        pe.wait_ge(turned_copied[2], j + 2)
                        pe.wait_ge(pq_read, j + 1)
                        for k in range(BB):
                            last = mm(node_pq[:, k * 2 * D:(k + 1) * 2 * D], x_tb[b][0:D + 1, k * P:(k + 1) * P],
                                      wt("pq", D + 1), start=k in (0, 4), stop=k in (3, BB - 1),
                                      skip_group_check=True)
                        last.then_inc(pq_done, 1)
                    if layer == 3:
                        pe.wait_ge(turned_copied[3], j + 2)
                        pe.wait_ge(batch_done[3], j + 1)
                        for k in range(BB):
                            last = mm(node_b[b][:, k, :], sx_t[b][0:D + 1, k * P:(k + 1) * P], wt("w4", D + 1),
                                      start=k == 0, stop=k == BB - 1, skip_group_check=True)
                        last.then_inc(y_done, 1)

                skewed(pe, multiply, turn)

        @block.scalar
        def _(act):
            copy = ACT.Copy
            for layer in range(4):
                act.sem_inc(turned_copied[layer], 1)
                if layer < 2:
                    act.sem_inc(counted[layer], 1)
            act.sem_inc(turn_copied, 2)
            act.sem_inc(pq_read, 1)
            act.wait_ge(w23_mm, 1)
            nc.scalar.activation(w23[:, :], pair[0][0:D + 1, 0:D], copy).then_inc(w23_ready, 1)
            act.wait_ge(cleared, 7)
            act.wait_ge(ld_w, 4 * COLS)
            act.wait_ge(flag_ready, 1)
            spread = act.value_load(flag_i[0:1, 0:1], min_val=0, max_val=1)

            for layer in range(4):
                if layer < 2:
                    with act.If(spread == 0):
                        for i, slots in gathered_groups(act, layer):
                            for b in slots:
                                n = 2 * i + b
                                act.wait_ge(z_used[layer], 2 * n + 4)
                                act.wait_ge(cwin_done[layer], n + 1)
                                for q in range(4):
                                    last = nc.scalar.activation(counts[:, b, HI[q][0] * W:HI[q][1] * W],
                                                                count_banks[q], copy)
                                last.then_inc(counted[layer], 1)
                if layer == 3:
                    with act.If(spread == 0):
                        with act.Fori(0, NG // 2) as i:
                            for b in range(2):
                                g = 2 * i + b
                                act.wait_ge(turn_done, g + 1)
                                act.wait_ge(zed_done, g + 1)
                                nc.scalar.activation(onehot_t[:, b, :], oh_t[b], copy).then_inc(turn_copied, 1)
                                act.wait_ge(z_summed, g + 3)
                                nc.scalar.activation(act_in[:, b, :, :], act_in[:, b, :, :], ACT.Silu)\
                                    .then_inc(silu_done, 1)
                    with act.Else():
                        with act.Fori(0, NG) as g:
                            act.wait_ge(g_sum, g + 2)
                            nc.scalar.activation(act_in[:, 0, :, :], act_in[:, 0, :, :], ACT.Silu).then_inc(g_silu, 1)

                def stage(j, b, i):
                    act.wait_ge(products[layer], j + 1)
                    act.nop(nofuse=True)
                    if layer in (0, 3):
                        nc.scalar.activation(x_tb[b][0:D, :], XT[:, bass.ds(j * BN, BN)], copy)
                    nc.scalar.activation(s_t[b][0:READ[layer], :], accT[0:READ[layer], bass.ds(j * BN, BN)], copy)\
                        .then_inc(staged[layer], 1)

                def bring(j, b, i):
                    if layer == 3:
                        act.wait_ge(products[3], j + 3)
                        act.wait_ge(y_done, j + 1)
                        nc.scalar.activation(u[b][:, :, :], node_a[b][:, :, 0:D], ACT.Silu).then_inc(u_done, 1)
                    act.wait_ge(turned[layer], j + 1)
                    act.nop(nofuse=True)
                    if layer < 2:
                        nc.scalar.activation(accT[0:D, bass.ds(j * BN, BN)], node_t[0:D, 0:BN], copy)\
                            .then_inc(turned_copied[layer], 1)
                    elif layer == 2:
                        act.wait_ge(pq_done, j + 1)
                        act.nop(nofuse=True)
                        nc.scalar.activation(XT[:, bass.ds(j * BN, BN)], node_t[0:D, 0:BN], copy)
                        nc.scalar.activation(x_tb[b][0:D, :], node_t[0:D, 0:BN], copy).then_inc(turned_copied[2], 1)
                        act.wait_ge(pq_done, j + 3)
                        act.wait_ge(slot_stored[3], j + 1)
                        pq = node_pq[:, 0:BB * 2 * D].rearrange("p (k c) -> p k c", k=BB)
                        nc.scalar.activation(tab[b][:, :, :], pq[:, :, 0:D], copy)
                        nc.scalar.activation(q_f[b][:, :, :], pq[:, :, D:2 * D], copy).then_inc(pq_read, 1)
                    else:
                        nc.scalar.activation(sx_t[b][0:D, :], node_t[0:D, 0:BN], copy).then_inc(turned_copied[3], 1)

                act.wait_ge(pass_done, layer + 1)
                skewed(act, stage, bring)

        @block.vector
        def _(dve):
            v = nc.vector
            tt, ts, stt = v.tensor_tensor, v.tensor_scalar, v.scalar_tensor_tensor
            link = Chain(dve, dve_step)
            for layer in range(4):
                dve.sem_inc(acc_added[layer], 2)
                if layer < 2:
                    dve.sem_inc(c_added[layer], 2)
                dve.sem_inc(g_free[layer], 1)
            dve.sem_inc(batch_done[3], 2)
            dve.sem_inc(z_summed, 2)
            dve.sem_inc(g_sum, 1)

            for b in range(2):
                v.memset(x_tb[b][D:D + 1, :], 1.0).then_inc(cleared, 1)
                v.memset(sx_t[b][D:D + 1, :], 1.0).then_inc(cleared, 1)
            dve.wait_ge(consts, 9)
            scratch = dst_rel[:, :].bitcast(I32)
            dve.wait_ge(ld_src, COLS)
            link(ts(scratch, edge_i[:, :], P - 1, None, ALU.bitwise_and))
            link(v.tensor_copy(src_lo[:, :], scratch))
            link(ts(scratch, edge_i[:, :], 7, None, ALU.logical_shift_right))
            v.tensor_copy(src_hi[:, :], scratch).then_inc(src_split, 1)
            dve.wait_ge(src_split, 1)
            dve.wait_ge(ld_first, 2 * COLS)
            link(v.tensor_copy(first_f[:, :], first_bc[:, :]))
            dve.wait_ge(ld_dst, COLS)
            link(v.tensor_copy(dst_rel[:, :], edge_i[:, :]))
            rel3 = dst_rel[:, :].rearrange("p (g t) -> p g t", t=TG)
            link(tt(rel3, rel3, along(first_f[:, :], TG), ALU.subtract))
            share3 = comb.rearrange("p (g t) -> p g t", t=TG)
            for t in range(TG):
                link(ts(share3[:, :, t], rel3[:, :, t], float(-SHARE[t]), None, ALU.add))
            link(v.tensor_reduce(span[:, 0:1], dst_rel[:, :], AX.X, ALU.max))
            link(v.tensor_reduce(span[:, 1:2], dst_rel[:, :], AX.X, ALU.min))
            link(v.tensor_reduce(span[:, 2:3], comb, AX.X, ALU.max))
            link(v.tensor_reduce(span[:, 3:4], comb, AX.X, ALU.min))
            link(ts(span[:, 0:1], span[:, 0:1], float(1 - W), None, ALU.add))
            link(stt(span[:, 0:1], span[:, 2:3], float(1 - WS), span[:, 0:1], ALU.add, ALU.max))
            link(tt(span[:, 1:2], span[:, 1:2], span[:, 3:4], ALU.min))
            stt(span[:, 4:5], span[:, 1:2], -1.0, span[:, 0:1], ALU.mult, ALU.max).then_inc(span_ready, 1)
            link(stt(comb, src_hi[:, :], float(WS), comb, ALU.mult, ALU.add))
            dve.wait_ge(span_turned, 1)
            link(v.tensor_reduce(flag_f[:, 0:1], pair[1][0:1, 0:P], AX.X, ALU.max))
            link(ts(flag_f[:, 1:2], flag_f[:, 0:1], 0.0, None, ALU.is_gt))
            v.tensor_copy(flag_i[:, :], flag_f[:, 1:2]).then_inc(flag_ready, 1)
            with dve.Fori(0, NG // 2) as i:
                for b in range(2):
                    g = 2 * i + b
                    dve.wait_ge(hist_mm, g + 1)
                    tt(hist_lo[:, b, :, :], iota_bc(P), along(cols(src_lo, g), P), ALU.is_equal)
                    tt(hist_hi[:, b, :, :], iota_bc(NB), along(cols(src_hi, g), NB), ALU.is_equal).then_inc(hist_oh, 1)
            dve.wait_ge(hist_mm, NG + 3)
            ts(r_out[:, :], hist, 1.0, None, ALU.max).then_inc(asked, 1)
            dve.wait_ge(rooted, 1)
            dve.wait_ge(ld_x, COLS)
            tt(X0, X[:, :, :], along(r_out[:, :], D), ALU.mult).then_inc(t0_ready, 1)
            dve.wait_ge(t0_ready, 1)
            link(v.tensor_copy(xparts[:, :, 0:D], X0))
            dve.wait_ge(stored[0][0], COLS)
            link(tt(X0, X0, xparts[:, :, 0:D], ALU.subtract))
            link(v.tensor_copy(xparts[:, :, D:2 * D], X0))
            link(tt(X0, X0, xparts[:, :, D:2 * D], ALU.subtract))
            v.tensor_copy(xparts[:, :, 2 * D:3 * D], X0).then_inc(parts_ready, 1)
            dve.wait_ge(parts_ready, 1)
            dve.wait_ge(ld_w, 4 * COLS)
            dve.wait_ge(cleared, 7)
            dve.wait_ge(flag_ready, 1)
            link.close()
            spread = dve.value_load(flag_i[0:1, 0:1], min_val=0, max_val=1)

            def norm(to, x, eps, n, done=None):
                link(v.tensor_reduce(c1[:, :], x, AX.X, ALU.add))
                link(stt(t1[:, :, :], along(c1[:, :], D), -1.0 / D, x, ALU.mult, ALU.add))
                link(tt(t2[:, :, :], t1[:, :, :], t1[:, :, :], ALU.mult))
                link(v.tensor_reduce(c1[:, :], t2[:, :, :], AX.X, ALU.add))
                ts(c2[:, 0, :], c1[:, :], 1.0 / D, float(eps), ALU.mult, ALU.add).then_inc(asked, 1)
                dve.wait_ge(rooted, n)
                last = tt(to, t1[:, :, :], along(c3[:, 0, :], D), ALU.mult)
                if done is None:
                    link(last)
                else:
                    last.then_inc(done, 1)

            for layer in range(4):
                m = SUMS[layer]
                if layer == 3:
                    for b in range(2):
                        v.memset(sx_t[b][D:D + 1, :], 1.0).then_inc(cleared, 1)
                    dve.wait_ge(cleared, 10)
                elif layer > 0:
                    dve.wait_ge(turned_copied[layer - 1], NBATCH + 1)
                with dve.If(spread == 0):
                    def add_window(g, bank_):
                        first = dve.value_load(first_i[0:1, bass.ds(g, 1)], min_val=0, max_val=NP - W)
                        sums = accT[0:m, bass.ds(first, W)]
                        return lambda: tt(sums, sums, bank_[0:m, :], ALU.add)

                    def mark_sources(n, b):
                        g = 2 * n + 1
                        dve.wait_ge(z_used[layer], 2 * n + 1)
                        tt(hist_lo[:, b, :, :], iota_bc(P), along(cols(src_lo, g), P), ALU.is_equal)
                        for t in range(TG):
                            if t % HALF == 0:
                                dve.wait_ge(z_used[layer], 2 * n + t // HALF + 1)
                            last = ts(zrows[:, t, 0:NH * WS], iota_z[:, :], comb[:, bass.ds(g * TG + t, 1)],
                                      None, ALU.is_equal)
                            if t % HALF == HALF - 1:
                                last.then_inc(z_ready[layer], 1)

                    def mark_targets(n, b):
                        g = 2 * n
                        dve.wait_ge(win_done[layer], n + 1)
                        dve.wait_ge(cwin_done[layer], n + 1)
                        last = tt(onehot[:, b, :, :], iota_bc(W), along(cols(dst_rel, g), W), ALU.is_equal)
                        if layer == 0:
                            v.tensor_copy(msg[:, b, :, D + 1], cols(weight_cols, g))
                            tt(onehot_c[:, b, :, :], iota_bc(W), along(cols(dst_rel, g + 1), W), ALU.is_equal)
                            last = v.tensor_copy(ones_w[:, b, :, D + 1], cols(weight_cols, g + 1))
                        last.then_inc(oh_ready[layer], 1)

                    def add_pair(n, b):
                        add = add_window(2 * n, win[b])
                        dve.wait_ge(win_done[layer], n + 3)
                        dve.wait_ge(c_added[layer], n + 2)
                        add().then_inc(acc_added[layer], 1)
                        first = dve.value_load(first_i[0:1, bass.ds(2 * n + 1, 1)], min_val=0, max_val=NP - W)
                        sums = accT[0:m, bass.ds(first, W)]
                        parts = accT[0:D, bass.ds(first, W)]
                        dve.wait_ge(cwin_done[layer], n + 3)
                        dve.wait_ge(acc_added[layer], n + 3)
                        tt(sums, sums, cwin_c[b][0:m, :], ALU.add).then_inc(c_part[layer], 1)
                        dve.wait_ge(c_part[layer], 2 * n + 1)
                        tt(parts, parts, cwin_ab[b][D:2 * D, :], ALU.add).then_inc(c_part[layer], 1)
                        dve.wait_ge(c_part[layer], 2 * n + 2)
                        tt(parts, parts, cwin_ab[b][0:D, :], ALU.add).then_inc(c_added[layer], 1)

                    if layer < 2:
                        def step(n, b):
                            mark_sources(n + 2, b)
                            add_pair(n, b)
                            mark_targets(n + 2, b)

                        for b in range(2):
                            mark_sources(b, b)
                            mark_targets(b, b)
                        with dve.Fori(0, (PAIRS - 2) // 2) as i:
                            step(2 * i, 0)
                            step(2 * i + 1, 1)
                        if PAIRS % 2:
                            step(PAIRS - 3, 0)
                        add_pair(PAIRS - 2, PAIRS % 2)
                        add_pair(PAIRS - 1, 1 - PAIRS % 2)
                        dve.wait_ge(c_added[layer], PAIRS + 2)
                    for i in two_by_two(dve, layer):
                        for b in range(2):
                            g = 2 * i + b
                            dve.wait_ge(win_done[layer], g + 1)
                            if layer == 2:
                                tt(onehot[:, b, :, :], iota_bc(W), along(cols(dst_rel, g), W), ALU.is_equal)\
                                    .then_inc(oh_raw, 1)
                                dve.wait_ge(oh_raw, g + 1)
                                tt(onehot[:, b, :, :], onehot[:, b, :, :], along(cols(weight_cols, g), W), ALU.mult)\
                                    .then_inc(oh_ready[2], 1)
                            else:
                                tt(onehot16[:, b, :, :], iota_bc(W), along(cols(dst_rel, g), W), ALU.is_equal)
                                tt(onehot[:, b, :, :], iota_bc(W), along(cols(dst_rel, g), W), ALU.is_equal)\
                                    .then_inc(oh_ready[3], 1)
                                dve.wait_ge(gathered[3][b], (i + 1) * COLS * TG)
                                dve.wait_ge(zed_done, g + 3)
                                tt(act_in[:, b, :, :], zed[b], msg[:, b, :, 0:D], ALU.add).then_inc(z_summed, 1)
                            first = dve.value_load(first_i[0:1, bass.ds(g, 1)], min_val=0, max_val=NP - W)
                            sums = accT[0:m, bass.ds(first, W)]
                            dve.wait_ge(win_done[layer], g + 3)
                            dve.wait_ge(acc_added[layer], g + 2)
                            tt(sums, sums, win[b][0:m, :], ALU.add).then_inc(acc_added[layer], 1)
                    if layer >= 2:
                        dve.wait_ge(acc_added[layer], NG + 2)
                with dve.Else():
                    with dve.Fori(0, NG) as g:
                        if layer == 0:
                            v.tensor_copy(msg[:, 0, :, D + 1], cols(weight_cols, g))
                        if layer == 3:
                            dve.wait_ge(g_gathered[3], (g + 1) * COLS * 2 * TG)
                            dve.wait_ge(g_zed, g + 2)
                            tt(act_in[:, 0, :, :], zed[0], msg[:, 0, :, 0:D], ALU.add).then_inc(g_part, 1)
                            dve.wait_ge(g_part, g + 1)
                            tt(act_in[:, 0, :, :], act_in[:, 0, :, :], q_rows[:, :, :], ALU.add).then_inc(g_sum, 1)
                        tt(rel_w[:, :], cols(dst_rel, g), first_f[:, bass.ds(g, 1)].broadcast_to((P, TG)), ALU.add)\
                            .then_inc(g_rel[layer], 1)
                        with dve.Fori(0, NW) as w:
                            n = g * NW + w
                            dve.wait_ge(g_rel[layer], n + g + 1)
                            tt(onehot[:, 0, :, :], iota_bc(W), along(rel_w[:, :], W), ALU.is_equal)\
                                .then_inc(g_raw if layer == 2 else g_oh[layer], 1)
                            if layer == 2:
                                dve.wait_ge(g_raw, n + 1)
                                tt(onehot[:, 0, :, :], onehot[:, 0, :, :], along(cols(weight_cols, g), W), ALU.mult)\
                                    .then_inc(g_oh[2], 1)
                            sums = accT[0:m, bass.ds(w * W, W)]
                            dve.wait_ge(g_win[layer], n + 1)
                            ts(rel_w[:, :], rel_w[:, :], float(-W), None, ALU.add).then_inc(g_rel[layer], 1)
                            tt(sums, sums, win[0][0:m, :], ALU.add).then_inc(g_added[layer], 1)
                            dve.wait_ge(g_added[layer], n + 1)
                        dve.sem_inc(g_free[layer], 1)
                dve.sem_inc(pass_done, 1)

                roots = ROOTS_BEFORE[layer]
                for_batch = {0: 8, 1: 16, 2: 8, 3: 13}[layer]
                with dve.Fori(0, NBATCH // 2) as i:
                    link.enter(i, 2 * for_batch)
                    for b in range(2):
                        j = 2 * i + b
                        blocks = bass.ds(j * BB, BB)
                        Xb, A = X[:, blocks, :], node_a[b][:, :, 0:D]
                        if layer == 0:
                            dve.wait_ge(staged[0], j + 1)
                            tt(sx_t[b][0:D + 1, :], s_t[b][0:D + 1, :], x_tb[b][0:D + 1, :], ALU.mult)\
                                .then_inc(sx_ready, 1)
                            dve.wait_ge(products[0], j + 3)
                            ts(c2[:, 0, :], node_a[b][:, :, D], 1.0, None, ALU.max)
                            ts(c2[:, 1, :], node_a[b][:, :, D], 1.0, None, ALU.add).then_inc(asked, 1)
                            v.tensor_copy(degrees[:, blocks, :], node_a[b][:, :, D:D + 2])
                            dve.wait_ge(rooted, roots + 2 * j + 1)
                            tt(t1[:, :, :], A, along(c3[:, 0, :], D), ALU.mult)
                            link(v.tensor_copy(dinv1[:, blocks], c3[:, 1, :]))
                            link(tt(t1[:, :, :], t1[:, :, :], node_b[b], ALU.add))
                            link(tt(t2[:, :, :], t1[:, :, :], Xb, ALU.add))
                            norm(Xb, t2[:, :, :], 1e-5, roots + 2 * j + 2)
                            dve.wait_ge(slot_stored[1], j + 1)
                            dve.wait_ge(split_done[0], j + 1)
                            tt(tab[b][:, :, :], Xb, along(dinv1[:, blocks], D), ALU.mult).then_inc(batch_done[0], 1)
                        elif layer == 1:
                            dve.wait_ge(products[1], j + 3)
                            link(tt(t1[:, :, :], A, along(dinv1[:, blocks], D), ALU.mult))
                            link(tt(t1[:, :, :], t1[:, :, :], row("b1"), ALU.add))
                            link(stt(t1[:, :, :], t1[:, :, :], 0.0, Xb, ALU.max, ALU.add))
                            norm(t2[:, :, :], t1[:, :, :], 1e-8, roots + 2 * j + 1)
                            link(tt(t2[:, :, :], t2[:, :, :], row("gamma1"), ALU.mult))
                            link(tt(t2[:, :, :], t2[:, :, :], row("beta1"), ALU.add))
                            link(tt(t2[:, :, :], t2[:, :, :], Xb, ALU.add))
                            norm(Xb, t2[:, :, :], 1e-5, roots + 2 * j + 2)
                            dve.wait_ge(slot_stored[2], j + 1)
                            tt(tab[b][:, :, :], Xb, along(dis2[:, blocks], D), ALU.mult).then_inc(batch_done[1], 1)
                        elif layer == 2:
                            dve.wait_ge(products[2], j + 3)
                            link(tt(t1[:, :, :], A, along(dis2[:, blocks], D), ALU.mult))
                            link(tt(t1[:, :, :], t1[:, :, :], row("b2"), ALU.add))
                            link(stt(t1[:, :, :], t1[:, :, :], 0.0, Xb, ALU.max, ALU.add))
                            norm(u[b][:, :, :], t1[:, :, :], 1e-5, roots + j + 1)
                            tt(Xb, t1[:, :, :], along(c3[:, 0, :], D), ALU.mult).then_inc(batch_done[2], 1)
                            dve.wait_ge(batch_done[2], j + 1)
                        else:
                            dve.wait_ge(y_done, j + 3)
                            link(tt(t1[:, :, :], node_b[b], Xb, ALU.add))
                            norm(t2[:, :, :], t1[:, :, :], 1e-5, roots + 2 * j + 1)
                            link(tt(t2[:, :, :], t2[:, :, :], row("gamma3"), ALU.mult))
                            link(tt(t2[:, :, :], t2[:, :, :], row("beta3"), ALU.add))
                            link(tt(t2[:, :, :], t2[:, :, :], Xb, ALU.add))
                            dve.wait_ge(slot_stored[4], j + 1)
                            norm(tab[b][:, :, :], t2[:, :, :], 1e-5, roots + 2 * j + 2, batch_done[3])
                            dve.wait_ge(batch_done[3], j + 3)
                link.leave(NBATCH // 2)
                if layer == 0:
                    link(ts(dis_a[:, :], degrees[:, :, 1], 1.0, None, ALU.add))
                    link(ts(dis_b[:, :], dis_a[:, :], 0.0, None, ALU.is_gt))
                    ts(dis_a[:, :], dis_a[:, :], TINY, None, ALU.max).then_inc(asked, 1)
                    dve.wait_ge(rooted, ROOTS_BEFORE[1])
                    link(tt(dis2[:, :], dis_a[:, :], dis_b[:, :], ALU.mult))
                    link.close()


def kernel(**inputs):
    import numpy as _np
    import concourse.bacc as _bacc
    from concourse import mybir as _mybir
    from concourse.bass_utils import run_bass_kernel_spmd as _run

    a = {name: _np.ascontiguousarray(x) for name, x in inputs.items()}
    n, e = a["x"].shape[0], a["src"].shape[0]
    n_pad, e_pad = shapes(n, e)
    NB, NG, f = n_pad // P, e_pad // GE, a["x"].dtype

    def edges(x, fill):
        full = _np.empty((e_pad,), x.dtype)
        full[:e] = x
        full[e:] = fill
        return _np.ascontiguousarray(full.reshape(NG * TG, P).T), full

    src_cols, _ = edges(a["src"], n)
    dst_cols, dst_full = edges(a["dst"], n + _np.arange(e_pad - e) * n // e)
    w_cols, _ = edges(a["edge_weight"], 0)
    dst_first = _np.ascontiguousarray(_np.broadcast_to(dst_full[::GE], (P, NG)))
    x_full = _np.zeros((n_pad, D), f)
    x_full[:n] = a["x"]
    x_nodes = _np.ascontiguousarray(x_full.reshape(NB, P, D).transpose(1, 0, 2))
    x_t = _np.ascontiguousarray(x_full.T)
    edge_full = _np.zeros((e_pad, DE), f)
    edge_full[:e] = a["edge_attr_32"]
    edge_t = _np.ascontiguousarray(edge_full.reshape(NG, 2, 4, P, DE).transpose(2, 4, 0, 1, 3).reshape(P, NG * 2, P))

    weights = _np.zeros((P, WCOLS), f)

    def put(name, at_row, at_col, x):
        at = WEIGHTS[name][0] + at_col
        weights[at_row:at_row + x.shape[0], at:at + x.shape[1]] = x

    one = _np.ones((1, 1), f)
    w1, w3 = a["L3_gnn_w1"], a["L3_gnn_w3"]
    for k in range(4):
        put("edge", k * DE, k * D, w1[2 * D:])
    put("wn", 0, 0, a["L0_gnn_Wn"].T)
    put("wn", D, 0, a["L0_gnn_bn"][None])
    put("wn", D, D, one)
    put("wn", D + 1, D + 1, one)
    put("wm", 0, 0, a["L0_gnn_Wm"].T)
    put("wm", D, 0, a["L0_gnn_bm"][None])
    put("xn", 0, 0, a["L0_gnn_Wn"].T)
    put("xn", D, 0, a["L0_gnn_bn"][None])
    put("w1", 0, 0, a["L1_gnn_W"])
    put("w2", 0, 0, a["L2_gnn_W"].T)
    put("pq", 0, 0, w1[:D])
    put("pq", D, 0, a["L3_gnn_b1"][None])
    put("pq", 0, D, w1[D:2 * D])
    put("w2t_b2", 0, 0, a["L3_gnn_w2"].T)
    put("w2t_b2", 0, D, a["L3_gnn_b2"][:, None])
    put("w3b", 0, 0, w3[D:])
    put("w3a", 0, 0, w3[:D])
    put("w3a", D, 0, a["L3_gnn_b3"][None])
    put("w4", 0, 0, a["L3_gnn_w4"])
    put("w4", D, 0, a["L3_gnn_b4"][None])
    rows = _np.stack([a[k] for k in ("L1_gnn_b", "L1_gnn_ln_gamma", "L1_gnn_ln_beta", "L2_gnn_b", "L3_gnn_gamma",
                                     "L3_gnn_beta")])
    rows = _np.ascontiguousarray(_np.broadcast_to(rows, (P,) + rows.shape))

    nc = _bacc.Bacc("TRN2", target_bir_lowering=False, num_devices=1)
    arrays, args = {}, []
    for name, x in (("x_nodes", x_nodes), ("x_t", x_t), ("src_cols", src_cols), ("dst_cols", dst_cols),
                    ("dst_first", dst_first), ("w_cols", w_cols), ("edge_t", edge_t), ("weights", weights),
                    ("rows", rows)):
        arrays[f"in_{name}"] = x
        args.append(nc.dram_tensor(f"in_{name}", x.shape, _mybir.dt.from_np(x.dtype), kind="ExternalInput").ap())
    args.append(nc.dram_tensor("out_nodes", (P, NB, D), _mybir.dt.from_np(f), kind="ExternalOutput").ap())
    gnn_program(nc, *args, n, e)
    r = _run(nc, [arrays], core_ids=[0])
    return _np.ascontiguousarray(r.results[0]["out_nodes"].transpose(1, 0, 2).reshape(n_pad, D)[:n])
```

```python
from contextlib import ExitStack

import concourse.bass as bass
from concourse import mybir

F32 = mybir.dt.float32
BF16 = mybir.dt.bfloat16
I32 = mybir.dt.int32
ALU = mybir.AluOpType
ACT = mybir.ActivationFunctionType
AX = mybir.AxisListType

P = 128
D = 64
DE = 32
TG = 8
GE = P * TG
W = 38
WS = 16
HALF = TG // 2
PATTERN = "GCCGCGC" * 2
BB = 5
COLS = 16
TINY = 1.1754944e-38


def padded(n, unit):
    return -(-n // unit) * unit


def shapes(n_nodes, n_edges):
    e_pad = padded(n_edges, 2 * GE)
    return padded(n_nodes + 1 + (e_pad - n_edges) * n_nodes // n_edges + W, 2 * BB * P), e_pad


WEIGHTS = {}
_at = 0
for _name, _cols in (("edge", 4 * D), ("wn", D + 2), ("wm", D), ("xn", D), ("w1", D), ("w2", D), ("pq", 2 * D),
                     ("w2t_b2", D + 1), ("w3b", D), ("w3a", D), ("w4", D)):
    WEIGHTS[_name] = (_at, _cols)
    _at += _cols
WCOLS = _at
ROWS = {name: k for k, name in enumerate(("b1", "gamma1", "beta1", "b2", "gamma3", "beta3"))}


class Chain:

    def __init__(self, engine, sem):
        self.engine, self.sem, self.done, self.base, self.n, self.per = engine, sem, 0, 0, 0, 0

    def enter(self, i, per):
        self.base, self.n, self.per = self.done + i * per, 0, per

    def leave(self, times):
        assert self.n == self.per, (self.n, self.per)
        self.done += times * self.per
        self.base, self.n = self.done, 0

    def __call__(self, ins):
        self.n += 1
        ins.then_inc(self.sem, 1)
        self.engine.wait_ge(self.sem, self.base + self.n)

    def two(self, step):
        for b in range(2):
            self.engine.wait_ge(self.sem, self.base + max(self.n - 1, 0))
            self.n += 1
            step(b).then_inc(self.sem, 1)

    def wait_own(self, b):
        self.engine.wait_ge(self.sem, self.base + self.n - 1 + b)

    def close(self):
        self.done += self.n
        self.base, self.n = self.done, 0


def gnn_program(nc, x_nodes, x_t, src_cols, dst_cols, dst_first, w_cols, edge_t, weights, rows, out, n_nodes, n_edges):
    NB = x_nodes.shape[1]
    NP = NB * P
    NG = src_cols.shape[1] // TG
    NW = -(-NP // W)
    NBATCH = NB // BB
    BN = BB * P
    ROUNDS, TAIL = NG // len(PATTERN), NG % len(PATTERN)
    PLACES = {kind: [k for k, x in enumerate(PATTERN) if x == kind] for kind in "GC"}
    TAILS = {kind: PATTERN[:TAIL].count(kind) for kind in "GC"}
    N_OF = {kind: ROUNDS * len(PLACES[kind]) + TAILS[kind] for kind in "GC"}
    assert min(TAILS.values()) >= 2
    TRIPLES = NG // 3
    REST = NG % 3
    NH = n_nodes // P + 1
    HI = [(NH * q // 4, NH * (q + 1) // 4) for q in range(4)]
    assert all((h1 - h0) * W <= 512 for h0, h1 in HI)

    SHARE = [min(max(round((t + 0.5) * P * n_nodes / n_edges - WS / 2), 0), W - WS) for t in range(TG)]
    SHARE[0], SHARE[-1] = 0, W - WS
    if any(b - a > WS for a, b in zip(SHARE, SHARE[1:])):
        SHARE = [t * (W - WS) // (TG - 1) for t in range(TG)]

    ctx = ExitStack()
    with ctx:
        def sb(name, shape, dt=F32):
            return ctx.enter_context(nc.sbuf_tensor(name, shape, dt))

        def ps(name, shape, dt=F32):
            return ctx.enter_context(nc.psum_tensor(name, shape, dt))

        def sem(name):
            return ctx.enter_context(nc.semaphore(name))

        table = [nc.dram_tensor(f"table{n}", (NP, D), F32, kind="Internal").ap() for n in range(4)]
        q_parts_dram = nc.dram_tensor("q_parts_dram", (NP, 3 * D), BF16, kind="Internal").ap()
        q_dram = nc.dram_tensor("q_dram", (NP, D), F32, kind="Internal").ap()

        X = sb("X", [P, NB, D])
        XT = sb("XT", [D, NP])
        accT = sb("accT", [D + 2, NW * W])
        weight_cols = sb("weight_cols", [P, NG * TG])
        edge_i = sb("edge_i", [P, NG * TG], I32)
        dst_rel = sb("dst_rel", [P, NG * TG])
        src_lo = sb("src_lo", [P, NG * TG], BF16)
        src_hi = sb("src_hi", [P, NG * TG], BF16)
        xparts = sb("xparts", [P, NB, 3 * D], BF16)
        first_i = sb("first_i", [1, NG], I32)
        first_bc = sb("first_bc", [P, NG], I32)
        first_f = sb("first_f", [P, NG])
        Wt = sb("Wt", [P, WCOLS])
        R = sb("R", [P, len(ROWS), D])
        w23 = sb("w23", [D + 1, D])
        ident = sb("ident", [P, P])
        ident16 = sb("ident16", [P, P], BF16)
        iota_z = sb("iota_z", [P, NH * WS], mybir.dt.float16)
        iota_f = sb("iota_f", [P, P])
        iota_t = sb("iota_t", [P, P, TG], BF16)
        zero16 = sb("zero16", [P, P], BF16)
        degrees = sb("degrees", [P, NB, 2])
        r_out = sb("r_out", [P, NB])
        dinv1 = sb("dinv1", [P, NB])
        dis2 = sb("dis2", [P, NB])
        dis_a = sb("dis_a", [P, NB])
        dis_b = sb("dis_b", [P, NB])
        span = sb("span", [P, 4])
        flag_i = sb("flag_i", [1, 1], I32)
        flag_f = sb("flag_f", [1, 2])

        idx = sb("idx", [P, 2, TG], I32)
        didx = sb("didx", [P, TG], I32)
        msg = sb("msg", [P, 2, TG, D + 2])
        act_in = sb("act_in", [P, 2, TG, D])
        q_rows = act_in[:, 1, :, :]
        edge_sb = sb("edge_sb", [P, 2, 2, P])
        q_win = sb("q_win", [W, 2, 3 * D], BF16)
        onehot = sb("onehot", [P, 2, TG, W])
        onehot16 = sb("onehot16", [P, 2, TG, W], BF16)
        onehot_t = sb("onehot_t", [W, 2, GE], BF16)
        hist_lo = sb("hist_lo", [P, 2, P, TG], BF16)
        hist_hi = sb("hist_hi", [P, 2, NB, TG], BF16)
        zrows = sb("zrows", [P, TG, NB * WS], BF16)
        X0 = zrows[:, :, :].rearrange("p t c -> p (t c)").bitcast(F32)[:, 0:NB * D].rearrange("p (k d) -> p k d", d=D)
        comb = edge_i[:, :].bitcast(F32)
        tile_steps = xparts[:, :, :].rearrange("p k c -> p (k c)").bitcast(F32)[:, 0:NG * (TG - 1)]
        counts = sb("counts", [P, 2, NH * W], BF16)
        xtab = xparts[:, :, :].rearrange("p k c -> p (k c)")[:, 0:NB * 2 * D].bitcast(F32)\
            .rearrange("p (k d) -> p k d", d=D)
        weight_sums = counts[:, :, :].rearrange("p b c -> p (b c)").bitcast(F32)
        lo_w = sb("lo_w", [P, TG, 3, P], BF16)
        lo_f = sb("lo_f", [P, TG])
        w_part = sb("w_part", [P, 2, TG], BF16)
        w_rest = sb("w_rest", [P, 2, TG])
        ones_w = sb("ones_w", [P, 2, TG, D + 2])
        onehot_c = sb("onehot_c", [P, 2, TG, W])
        rel_w = sb("rel_w", [P, TG])

        s_t = [sb(f"s_t{b}", [D + 2, BN]) for b in range(2)]
        x_tb = [sb(f"x_tb{b}", [D + 1, BN]) for b in range(2)]
        sx_t = [sb(f"sx_t{b}", [D + 1, BN]) for b in range(2)]
        u = [sb(f"u{b}", [P, BB, D]) for b in range(2)]
        tab = [sb(f"tab{b}", [P, BB, D]) for b in range(2)]
        q_f = [sb(f"q_f{b}", [P, BB, D]) for b in range(2)]
        q_s = [xparts[:, b * BB:(b + 1) * BB, :] for b in range(2)]
        q_rest = sb("q_rest", [P, BB, D])
        t1 = [sb(f"t1{b}", [P, BB, D]) for b in range(2)]
        t2 = [sb(f"t2{b}", [P, BB, D]) for b in range(2)]
        c1 = [sb(f"c1{b}", [P, BB]) for b in range(2)]
        c2 = [sb(f"c2{b}", [P, 2, BB]) for b in range(2)]
        c3 = [sb(f"c3{b}", [P, 2, BB]) for b in range(2)]
        minus_half = sb("minus_half", [P, NB])

        bank = [ps(f"bank{n}", [P, 512]) for n in range(4)]
        pair = [ps(f"pair{n}", [P, 1024]) for n in range(2)]
        win = [bank[b][:, 0:W] for b in range(2)]
        cwin_ab = [bank[2 + b][:, 0:W] for b in range(2)]
        cwin_c = [bank[2 + b][:, 64:64 + W] for b in range(2)]
        count_banks = [pair[q // 2][:, 512 * (q % 2):512 * (q % 2) + (HI[q][1] - HI[q][0]) * W] for q in range(4)]
        zed = [bank[2 + b][:, :].rearrange("p (t d) -> p t d", t=TG) for b in range(2)]
        oh_t = [pair[b][0:W, 0:512].bitcast(BF16) for b in range(2)]
        node_a = [bank[2 + b][:, 0:BB * (D + 2)].rearrange("p (k d) -> p k d", k=BB) for b in range(2)]
        node_b = [pair[0][:, 512 * b:512 * b + BB * D].rearrange("p (k d) -> p k d", k=BB) for b in range(2)]
        node_pq = pair[0]
        node_t = pair[1]
        hist = bank[0][:, 0:NB]

        ld_x, ld_src, ld_dst, ld_first, ld_w = (sem(n) for n in ("ld_x", "ld_src", "ld_dst", "ld_first", "ld_w"))
        consts, dve_step, src_split = sem("consts"), sem("dve_step"), sem("src_split")
        hist_oh, hist_mm = sem("hist_oh"), sem("hist_mm")
        span_ready, span_turned, flag_ready = sem("span_ready"), sem("span_turned"), sem("flag_ready")
        w23_mm, w23_ready, t0_ready, cleared = sem("w23_mm"), sem("w23_ready"), sem("t0_ready"), sem("cleared")

        def per_layer(name, layers=range(4)):
            return {n: sem(f"{name}_{n}") for n in layers}

        def per_slot(name, layers=range(4)):
            return {n: [sem(f"{name}_{n}{b}") for b in range(2)] for n in layers}

        idx_in = {n: [sem(f"idx_in_{n}{b}") for b in range(2)] for n in range(4)}
        gathered = {n: [sem(f"gathered_{n}{b}") for b in range(2)] for n in range(4)}
        z_ready, z_used, counted = (per_layer(n, (0, 1, 2)) for n in ("z_ready", "z_used", "counted"))
        cwin_done, c_added = per_layer("cwin_done", (0, 1, 2)), per_layer("c_added", (0, 1, 2))
        c_part, w_split = sem("c_part"), sem("w_split")
        parts_ready, ones_ready = sem("parts_ready"), sem("ones_ready")
        oh_raw = sem("oh_raw")
        oh_ready, win_done, acc_added = per_layer("oh_ready"), per_layer("win_done"), per_layer("acc_added")
        edge_in, q_in = [sem(f"edge_in{b}") for b in range(2)], [sem(f"q_in{b}") for b in range(2)]
        turn_done, turn_copied, zed_done = sem("turn_done"), sem("turn_copied"), sem("zed_done")
        z_summed, silu_done = sem("z_summed"), sem("silu_done")
        g_idx, g_gathered, g_free = per_layer("g_idx"), per_layer("g_gathered"), per_layer("g_free")
        g_rel, g_raw, g_oh = per_layer("g_rel"), sem("g_raw"), per_layer("g_oh")
        g_win, g_added = per_layer("g_win"), per_layer("g_added")
        g_edge, g_zed, g_part, g_sum, g_silu = (sem(n) for n in ("g_edge", "g_zed", "g_part", "g_sum", "g_silu"))
        pass_done = sem("pass_done")
        a_read = sem("a_read")
        asked, rooted = sem("asked"), sem("rooted")
        normed = sem("normed")
        staged, products, batch_done = per_layer("staged"), per_layer("products"), per_layer("batch_done")
        turned, turned_copied = per_layer("turned"), per_layer("turned_copied")
        sx_ready, pq_done, pq_read = (sem(n) for n in ("sx_ready", "pq_done", "pq_read"))
        split_done, split_step = per_layer("split_done", (0, 1, 2)), per_layer("split_step", (0, 2))
        u_done, y_done = sem("u_done"), sem("y_done")
        stored = per_slot("stored")
        stored[4] = [sem(f"stored_4{b}") for b in range(2)]

        slot_stored = per_layer("slot_stored", (1, 2, 3, 4))

        STORES = {1: 1, 2: 1, 3: 3, 4: 1}

        def wt(name, k=D):
            at, cols = WEIGHTS[name]
            return Wt[0:k, at:at + cols]

        def row(name, n=BB):
            return R[:, ROWS[name], :].rearrange("p (k d) -> p k d", k=1).broadcast_to((P, n, D))

        def cols(t, g, n=TG):
            return t[:, bass.ds(g * TG, n)]

        def along(ap, n):
            return ap.rearrange("p (k o) -> p k o", o=1).broadcast_to((P, ap.shape[1], n))

        def across(t, g, n):
            return cols(t, g).rearrange("p (o k) -> p o k", o=1).broadcast_to((P, n, TG))

        def iota_bc(n, k=TG):
            return iota_f[:, 0:n].rearrange("p (k n) -> p k n", k=1).broadcast_to((P, k, n))

        SUMS = {0: D + 2, 1: D, 2: D, 3: D}
        READ = {0: D + 2, 1: D, 2: D, 3: D + 1}
        ROOTS = {0: 2, 1: 2, 2: 1, 3: 2}
        ROOTS_BEFORE = {0: 1}
        for layer in (1, 2, 3):
            ROOTS_BEFORE[layer] = ROOTS_BEFORE[layer - 1] + ROOTS[layer - 1] * NBATCH + (layer == 1)

        def group_of(kind, i, a):
            places = PLACES[kind]
            return (i + a // len(places)) * len(PATTERN) + places[a % len(places)]

        def rounds(eng, kinds="GC"):
            def one_round(i, items, tail):
                seen = {"G": 0, "C": 0}
                for kind in items:
                    a = seen[kind]
                    seen[kind] += 1
                    if kind in kinds:
                        yield kind, i, a, i * len(PLACES[kind]) + a, tail

            with eng.Fori(0, ROUNDS) as i:
                yield from one_round(i, PATTERN, False)
            yield from one_round(ROUNDS, PATTERN[:TAIL], True)

        def gathered_groups(eng, layer):
            if layer < 2:
                for _, i, a, n, _ in rounds(eng, "G"):
                    yield n, a % 2, i * (len(PLACES["G"]) // 2) + a // 2, group_of("G", i, a)
                return
            uses = 2 * TRIPLES + REST if layer == 2 else NG
            with eng.Fori(0, uses // 2) as i:
                for b in range(2):
                    yield 2 * i + b, b, i, (3 if layer == 2 else 2) * i + b
            if uses % 2:
                yield uses - 1, 0, uses // 2, (3 if layer == 2 else 2) * (uses // 2)

        def two_by_two(eng, layer):
            if layer == 3:
                with eng.Fori(0, NG // 2) as i:
                    yield i

        def skewed(eng, first, second):
            first(0, 0, 0)
            with eng.Fori(0, NBATCH // 2 - 1) as i:
                first(2 * i + 1, 1, i)
                second(2 * i, 0, i)
                first(2 * i + 2, 0, i + 1)
                second(2 * i + 1, 1, i)
            first(NBATCH - 1, 1, NBATCH // 2 - 1)
            second(NBATCH - 2, 0, NBATCH // 2 - 1)
            second(NBATCH - 1, 1, NBATCH // 2 - 1)

        def pairwise(eng, first, second):
            for b in range(2):
                first(b, b, 0)
            with eng.Fori(0, NBATCH // 2 - 1) as i:
                for b in range(2):
                    first(2 * i + 2 + b, b, i + 1)
                for b in range(2):
                    second(2 * i + b, b, i)
            for b in range(2):
                second(NBATCH - 2 + b, b, NBATCH // 2 - 1)

        block = ctx.enter_context(nc.Block())

        @block.sync
        def _(sp):
            sp.dma_start(edge_i[:, :], src_cols).then_inc(ld_src, COLS)
            sp.dma_start(first_i[:, :], dst_first[0:1, :]).then_inc(ld_first, COLS)
            sp.dma_start(first_bc[:, :], dst_first).then_inc(ld_first, COLS)
            sp.dma_start(X[:, :, :], x_nodes).then_inc(ld_x, COLS)
            sp.wait_ge(src_split, 1)
            sp.dma_start(edge_i[:, :], dst_cols).then_inc(ld_dst, COLS)
            sp.dma_start(Wt[:, :], weights).then_inc(ld_w, COLS)
            sp.dma_start(R[:, :, :], rows).then_inc(ld_w, COLS)
            sp.dma_start(weight_cols[:, :], w_cols).then_inc(ld_w, COLS)
            sp.dma_start(XT[:, :], x_t).then_inc(ld_w, COLS)
            for n in (1, 2, 3, 4):
                sp.sem_inc(slot_stored[n], 2)
            sp.wait_ge(t0_ready, 1)
            sp.dma_start(table[0].rearrange("(k p) d -> p k d", p=P), X0).then_inc(stored[0][0], COLS)
            sp.wait_ge(flag_ready, 1)
            spread = sp.value_load(flag_i[0:1, 0:1], min_val=0, max_val=1)

            for layer in range(4):
                if layer == 3:
                    for b in range(2):
                        sp.wait_ge(stored[3][b], COLS * STORES[3] * (NBATCH // 2))
                with sp.If(spread == 0):
                    for n, b, i, g in gathered_groups(sp, layer):
                        sp.wait_ge(z_summed if layer == 3 else win_done[layer], n + 1)
                        sp.dma_start(idx[:, b, :], cols(src_cols, g)).then_inc(idx_in[layer][b], COLS)
                        if layer == 3:
                            first = sp.value_load(first_i[0:1, bass.ds(g, 1)], min_val=0, max_val=NP - W)
                            sp.wait_ge(zed_done, g + 1)
                            sp.dma_start(edge_sb[:, b, :, :], edge_t[:, bass.ds(g * 2, 2), :])\
                              .then_inc(edge_in[b], COLS)
                            sp.dma_start(q_win[:, b, :], q_parts_dram[bass.ds(first, W), :])\
                              .then_inc(q_in[b], COLS)
                with sp.Else():
                    with sp.Fori(0, NG) as g:
                        sp.wait_ge(g_free[layer], g + 1)
                        sp.dma_start(idx[:, 0, :], cols(src_cols, g)).then_inc(g_idx[layer], COLS)
                        if layer == 3:
                            sp.dma_start(didx[:, :], cols(dst_cols, g)).then_inc(g_idx[layer], COLS)
                            sp.wait_ge(g_zed, g + 1)
                            sp.dma_start(edge_sb[:, 0, :, :], edge_t[:, bass.ds(g * 2, 2), :]).then_inc(g_edge, COLS)

                with sp.Fori(0, NBATCH // 2) as i:
                    for b in range(2):
                        j = 2 * i + b
                        of_batch = bass.ds(j * BN, BN)
                        if layer < 2:
                            sp.wait_ge(batch_done[layer], j + 1)
                            sp.dma_start(table[layer + 1][of_batch, :].rearrange("(k p) d -> p k d", p=P),
                                         tab[b][:, :, :]).then_inc(stored[layer + 1][b], COLS)
                        elif layer == 2:
                            sp.wait_ge(pq_read, j + 2)
                            sp.dma_start(table[3][of_batch, :].rearrange("(k p) d -> p k d", p=P),
                                         tab[b][:, :, :]).then_inc(stored[3][b], COLS)
                            sp.dma_start(q_dram[of_batch, :].rearrange("(k p) d -> p k d", p=P),
                                         q_f[b][:, :, :]).then_inc(stored[3][b], COLS)
                            sp.wait_ge(split_done[2], j + 1)
                            sp.dma_start(q_parts_dram[of_batch, :].rearrange("(k p) d -> p k d", p=P),
                                         q_s[b]).then_inc(stored[3][b], COLS)
                        else:
                            sp.wait_ge(batch_done[3], j + 3)
                            sp.dma_start(out[:, bass.ds(j * BB, BB), :], tab[b][:, :, :]).then_inc(stored[4][b], COLS)
                        sp.wait_ge(stored[layer + 1][b], COLS * STORES[layer + 1] * (i + 1))
                        sp.sem_inc(slot_stored[layer + 1], 1)
            for b in range(2):
                sp.wait_ge(stored[4][b], COLS * (NBATCH // 2))

        @block.gpsimd
        def _(pool):
            pool.memset(ident[:, :], 0.0).then_inc(consts, 1)
            pool.memset(ident16[:, :], 0.0).then_inc(consts, 1)
            pool.iota(iota_f[:, :], pattern=[[1, P]], base=0, channel_multiplier=0,
                      allow_small_or_imprecise_dtypes=True).then_inc(consts, 1)
            pool.iota(iota_t[:, :, :], pattern=[[1, P], [0, TG]], base=0, channel_multiplier=0,
                      allow_small_or_imprecise_dtypes=True).then_inc(consts, 1)
            pool.iota(iota_z[:, :], pattern=[[1, NH * WS]], base=0, channel_multiplier=0,
                      allow_small_or_imprecise_dtypes=True).then_inc(consts, 1)
            pool.memset(ones_w[:, :, :, 0:D], 0.0).then_inc(consts, 1)
            pool.memset(ones_w[:, :, :, D:D + 2], 1.0).then_inc(consts, 1)
            pool.memset(zero16[:, :], 0.0).then_inc(consts, 1)
            pool.wait_ge(consts, 8)
            for m in (ident, ident16):
                pool.affine_select(out=m[:, :], in_=m[:, :], compare_op=ALU.not_equal, fill=1.0, base=0,
                                   pattern=[[-1, P]], channel_multiplier=1).then_inc(consts, 1)
            pool.memset(minus_half[:, :], -0.5).then_inc(cleared, 1)
            pool.memset(msg[:, :, :, :], 1.0).then_inc(cleared, 1)
            pool.memset(accT[:, :], 0.0).then_inc(cleared, 1)
            pool.wait_ge(cleared, 7)
            for n in (0, 1):
                pool.sem_inc(split_done[n], 2)
            pool.wait_ge(asked, 1)
            pool.tensor_tensor(r_out[:, :], r_out[:, :], minus_half[:, :], ALU.pow).then_inc(rooted, 1)
            pool.wait_ge(flag_ready, 1)
            spread = pool.value_load(flag_i[0:1, 0:1], min_val=0, max_val=1)

            def gather(buf, rows_of, at, done):
                for t in range(TG):
                    pool.indirect_dma_start(out=buf[:, t, 0:D], out_offset=None, in_=rows_of,
                                            in_offset=bass.IndirectOffsetOnAxis(ap=at[:, t:t + 1], axis=0))\
                        .then_inc(done, COLS)

            for layer in range(4):
                if layer == 0:
                    pool.wait_ge(stored[0][0], COLS)
                else:
                    for b in range(2):
                        pool.wait_ge(stored[layer][b], COLS * STORES[layer] * (NBATCH // 2))
                with pool.If(spread == 0):
                    for n, b, i, g in gathered_groups(pool, layer):
                        pool.wait_ge(idx_in[layer][b], (i + 1) * COLS)
                        pool.wait_ge(z_summed if layer == 3 else win_done[layer], n + 1)
                        pool.nop(nofuse=True)
                        gather(msg[:, b, :, :], table[layer], idx[:, b, :], gathered[layer][b])
                with pool.Else():
                    with pool.Fori(0, NG) as g:
                        pool.wait_ge(g_idx[layer], (g + 1) * COLS * (2 if layer == 3 else 1))
                        pool.wait_ge(g_free[layer], g + 1)
                        pool.nop(nofuse=True)
                        gather(msg[:, 0, :, :], table[layer], idx[:, 0, :], g_gathered[layer])
                        if layer == 3:
                            gather(q_rows[:, :, :], q_dram, didx[:, :], g_gathered[layer])

                def roots(i, k):
                    for b in range(2):
                        two = slice(0, 2 if layer == 0 and k == 0 else 1)
                        pool.wait_ge(asked, ROOTS_BEFORE[layer] + 2 * (ROOTS[layer] * i + k) + b + 1)
                        pool.tensor_tensor(c3[b][:, two, :], c2[b][:, two, :], minus_half[:, 0:BB * two.stop]
                                           .rearrange("p (o k) -> p o k", k=BB), ALU.pow).then_inc(rooted, 1)

                def split(j, b, i):
                    if layer == 3:
                        return
                    if layer == 1:
                        pool.wait_ge(batch_done[1], j + 1)
                        pool.nop(nofuse=True)
                        pool.tensor_copy(xtab[:, bass.ds(j * BB, BB), :], tab[b][:, :, :]).then_inc(split_done[1], 1)
                        return
                    if layer == 0:
                        rows_in, parts = tab[b], xparts[:, bass.ds(j * BB, BB), :]
                        pool.wait_ge(batch_done[0], j + 1)
                    else:
                        rows_in, parts = q_f[b], q_s[b]
                        pool.wait_ge(pq_read, j + 2)
                        pool.wait_ge(slot_stored[3], j + 1)
                    step = split_step[layer]
                    pool.nop(nofuse=True)
                    pool.tensor_copy(parts[:, :, 0:D], rows_in[:, :, :]).then_inc(step, 1)
                    pool.wait_ge(step, 3 * j + 1)
                    pool.nop(nofuse=True)
                    pool.tensor_tensor(q_rest[:, :, :], rows_in[:, :, :], parts[:, :, 0:D], ALU.subtract)\
                        .then_inc(step, 1)
                    pool.wait_ge(step, 3 * j + 2)
                    pool.nop(nofuse=True)
                    pool.tensor_copy(parts[:, :, D:2 * D], q_rest[:, :, :]).then_inc(step, 1)
                    pool.wait_ge(step, 3 * j + 3)
                    pool.nop(nofuse=True)
                    pool.tensor_tensor(parts[:, :, 2 * D:3 * D], q_rest[:, :, :], parts[:, :, D:2 * D], ALU.subtract)\
                        .then_inc(split_done[layer], 1)
                    pool.wait_ge(split_done[layer], j + (3 if layer == 0 else 1))

                for k in range(ROOTS[layer]):
                    roots(0, k)
                with pool.Fori(0, NBATCH // 2 - 1) as i:
                    roots(i + 1, 0)
                    for b in range(2):
                        split(2 * i + b, b, i)
                    if ROOTS[layer] > 1:
                        roots(i + 1, 1)
                for b in range(2):
                    split(NBATCH - 2 + b, b, NBATCH // 2 - 1)
                if layer == 0:
                    pool.wait_ge(asked, ROOTS_BEFORE[1])
                    pool.tensor_tensor(dis_a[:, :], dis_a[:, :], minus_half[:, :], ALU.pow).then_inc(rooted, 1)
                if layer == 2:
                    pool.wait_ge(staged[2], NBATCH)
                    pool.memset(accT[0:D, :], 0.0).then_inc(cleared, 1)

        @block.tensor
        def _(pe):
            mm = nc.tensor.matmul
            for layer in range(4):
                pe.sem_inc(win_done[layer], 2)
                if layer < 3:
                    pe.sem_inc(z_used[layer], 2)
                    pe.sem_inc(cwin_done[layer], 2 if layer < 2 else 1)
                pe.sem_inc(products[layer], 2)
                pe.sem_inc(turned[layer], 2)
            for s, n in ((hist_mm, 2), (zed_done, 2), (g_zed, 1), (pq_done, 2), (y_done, 2)):
                pe.sem_inc(s, n)
            pe.wait_ge(consts, 10)
            mm(hist, zero16[:, :], zero16[:, 0:NB], start=True, stop=False)
            with pe.Fori(0, NG // 2) as i:
                for b in range(2):
                    pe.wait_ge(hist_oh, 2 * i + b + 1)
                    for t in range(TG):
                        last = mm(hist, hist_lo[:, b, :, t], hist_hi[:, b, :, t], start=False, stop=False)
                    last.then_inc(hist_mm, 1)
            mm(hist, zero16[:, :], zero16[:, 0:NB], start=False, stop=True).then_inc(hist_mm, 1)
            pe.wait_ge(ld_w, 4 * COLS)
            mm(pair[0][0:D + 1, 0:D], wt("w2t_b2"), wt("w3b"), start=True, stop=True).then_inc(w23_mm, 1)
            pe.wait_ge(span_ready, 1)
            nc.tensor.transpose(pair[1][0:1, 0:P], span[:, 3:4], ident[:, :]).then_inc(span_turned, 1)
            pe.wait_ge(w23_ready, 1)
            pe.wait_ge(cleared, 7)
            pe.wait_ge(flag_ready, 1)
            spread = pe.value_load(flag_i[0:1, 0:1], min_val=0, max_val=1)

            def scatter(layer, b, src):
                m = SUMS[layer]
                for t in range(TG):
                    last = mm(win[b][0:m, :], src[:, t, 0:m], onehot[:, b, t, :], start=t == 0, stop=t == TG - 1)
                return last

            def edge_products(b, stop):
                for h in range(2):
                    last = mm(zed[b][:, 4 * h:4 * h + 4, :].rearrange("p t d -> p (t d)"), edge_sb[:, b, h, :],
                              wt("edge", P), start=h == 0, stop=stop, skip_group_check=True)
                return last

            for layer in range(4):
                with pe.If(spread == 0):
                    def count(n, b):
                        pe.wait_ge(counted[layer], n + 1)
                        for t in range(TG):
                            if t % HALF == 0:
                                pe.wait_ge(z_ready[layer], 2 * n + t // HALF + 1)
                            for q in range(4):
                                to = count_banks[q].rearrange("p (h w) -> p h w", w=W)[:, :, SHARE[t]:SHARE[t] + WS]
                                last = mm(to, hist_lo[:, b, :, t], zrows[:, t, HI[q][0] * WS:HI[q][1] * WS],
                                          start=t == 0, stop=t == TG - 1, skip_group_check=True)
                            if t % HALF == HALF - 1:
                                last.then_inc(z_used[layer], 1)

                    def sum_one_gathered(n, b, uses):
                        pe.wait_ge(gathered[layer][b], (uses + 1) * COLS * TG)
                        pe.wait_ge(oh_ready[layer], n + 1)
                        pe.wait_ge(acc_added[layer], n + 1)
                        scatter(layer, b, msg[:, b, :, :]).then_inc(win_done[layer], 1)

                    def sum_one_counted(n, b):
                        if layer == 0:
                            pe.wait_ge(parts_ready, 1)
                            pe.wait_ge(ones_ready, n + 1)
                        else:
                            pe.wait_ge(split_done[0], NBATCH + 2)
                        pe.wait_ge(counted[layer], n + 2)
                        pe.wait_ge(c_added[layer], n + 1)
                        for h in range(NH):
                            of_h = counts[:, b, h * W:(h + 1) * W]
                            mm(cwin_ab[b], xparts[:, h, 0:2 * D], of_h, start=h == 0, stop=h == NH - 1,
                               skip_group_check=True)
                            last = mm(cwin_c[b][0:D, :], xparts[:, h, 2 * D:3 * D], of_h, start=False,
                                      stop=h == NH - 1, skip_group_check=True)
                        if layer == 0:
                            for t in range(TG):
                                last = mm(cwin_c[b][0:D + 2, :], ones_w[:, b, t, :], onehot_c[:, b, t, :],
                                          start=False, stop=t == TG - 1, skip_group_check=True)
                        last.then_inc(cwin_done[layer], 1)

                    def add_up_weights(n):
                        pe.wait_ge(counted[2], n + 1)
                        for t in range(TG):
                            if t % HALF == 0:
                                pe.wait_ge(z_ready[2], 2 * n + t // HALF + 1)
                            for q in range(4):
                                to = count_banks[q].rearrange("p (h w) -> p h w", w=W)[:, :, SHARE[t]:SHARE[t] + WS]
                                for p in range(3):
                                    last = mm(to, lo_w[:, t, p, :], zrows[:, t, HI[q][0] * WS:HI[q][1] * WS],
                                              start=t == 0 and p == 0, stop=t == TG - 1 and p == 2,
                                              skip_group_check=True)
                            if t % HALF == HALF - 1:
                                last.then_inc(z_used[2], 1)

                    def sum_gathered(n, s):
                        pe.wait_ge(gathered[2][s], (n + 1) * COLS * TG)
                        pe.wait_ge(oh_ready[2], 2 * n + s + 1)
                        pe.wait_ge(acc_added[2], 2 * n + s + 1)
                        scatter(2, s, msg[:, s, :, :]).then_inc(win_done[2], 1)

                    def sum_counted(n):
                        pe.wait_ge(split_done[1], NBATCH + 2)
                        pe.wait_ge(counted[2], n + 2)
                        pe.wait_ge(c_added[2], n + 1)
                        for h in range(NH):
                            last = mm(cwin_ab[0][0:D, :], xtab[:, h, :], weight_sums[:, h * W:(h + 1) * W],
                                      start=h == 0, stop=h == NH - 1)
                        last.then_inc(cwin_done[2], 1)

                    if layer < 2:
                        count(0, 0)
                        for kind, i, a, n, tail in rounds(pe):
                            if kind == "G":
                                sum_one_gathered(n, a % 2, i * (len(PLACES["G"]) // 2) + a // 2)
                            else:
                                if not tail or a + 1 < TAILS["C"]:
                                    count(n + 1, (a + 1) % 2)
                                sum_one_counted(n, a % 2)
                    if layer == 2:
                        add_up_weights(0)
                        with pe.Fori(0, TRIPLES - 1) as n:
                            sum_gathered(n, 0)
                            add_up_weights(n + 1)
                            sum_gathered(n, 1)
                            sum_counted(n)
                        sum_gathered(TRIPLES - 1, 0)
                        sum_gathered(TRIPLES - 1, 1)
                        sum_counted(TRIPLES - 1)
                        for s in range(REST):
                            sum_gathered(TRIPLES, s)
                    for i in two_by_two(pe, layer):
                        for b in range(2):
                            g = 2 * i + b
                            pe.wait_ge(oh_ready[3], g + 1)
                            pe.wait_ge(turn_copied, g + 1)
                            pe.nop(nofuse=True)
                            for t in range(TG):
                                last = nc.tensor.transpose(oh_t[b][:, t * P:(t + 1) * P],
                                                           onehot16[:, b, t, :], ident16[:, :])
                            last.then_inc(turn_done, 1)
                            pe.wait_ge(edge_in[b], (i + 1) * COLS)
                            pe.wait_ge(z_summed, g + 1)
                            edge_products(b, False)
                            pe.wait_ge(q_in[b], (i + 1) * COLS)
                            pe.wait_ge(turn_copied, g + 3)
                            for t in range(TG):
                                for p in range(3):
                                    last = mm(zed[b][:, t, :], onehot_t[:, b, t * P:(t + 1) * P],
                                              q_win[:, b, p * D:(p + 1) * D], start=False, stop=p == 2,
                                              skip_group_check=True)
                            last.then_inc(zed_done, 1)
                            pe.wait_ge(silu_done, g + 1)
                            pe.wait_ge(acc_added[3], g + 1)
                            scatter(3, b, act_in[:, b, :, :]).then_inc(win_done[3], 1)
                with pe.Else():
                    with pe.Fori(0, NG) as g:
                        if layer == 3:
                            pe.wait_ge(g_edge, (g + 1) * COLS)
                            pe.wait_ge(g_sum, g + 1)
                            edge_products(0, True).then_inc(g_zed, 1)
                            pe.wait_ge(g_silu, g + 1)
                        else:
                            pe.wait_ge(g_gathered[layer], (g + 1) * COLS * TG)
                        pe.nop(nofuse=True)
                        with pe.Fori(0, NW) as w:
                            pe.wait_ge(g_oh[layer], g * NW + w + 1)
                            scatter(layer, 0, act_in[:, 0, :, :] if layer == 3 else msg[:, 0, :, :])\
                                .then_inc(g_win[layer], 1)

                def multiply(j, b, i):
                    pe.wait_ge(sx_ready if layer == 0 else staged[layer], j + 1)
                    if layer < 3:
                        pe.wait_ge(a_read, layer * NBATCH + j + 1)
                        pe.nop(nofuse=True)
                    for k in range(BB):
                        n = slice(k * P, (k + 1) * P)
                        to, ends = node_a[b][:, k, 0:D], k == BB - 1
                        if layer == 0:
                            mm(node_a[b][:, k, :], s_t[b][0:D + 2, n], wt("wn", D + 2), start=k == 0, stop=False,
                               skip_group_check=True)
                            mm(to, sx_t[b][0:D + 1, n], wt("wm", D + 1), start=False, stop=ends,
                               skip_group_check=True)
                            last = mm(node_b[b][:, k, :], x_tb[b][0:D + 1, n], wt("xn", D + 1), start=k == 0,
                                      stop=ends, skip_group_check=True)
                        elif layer == 3:
                            mm(to, s_t[b][0:D + 1, n], w23[:, :], start=k == 0, stop=False, skip_group_check=True)
                            last = mm(to, x_tb[b][0:D + 1, n], wt("w3a", D + 1), start=False, stop=ends,
                                      skip_group_check=True)
                        else:
                            last = mm(to, s_t[b][0:D, n], wt("w1" if layer == 1 else "w2"), start=k == 0,
                                      stop=ends, skip_group_check=True)
                    last.then_inc(products[layer], 1)

                def turn(j, b, i):
                    pe.wait_ge(u_done if layer == 3 else batch_done[layer], j + 1)
                    pe.wait_ge(turned_copied[layer], j + 1)
                    pe.nop(nofuse=True)
                    rows_in = (u if layer >= 2 else tab)[b]
                    for k in range(BB):
                        last = nc.tensor.transpose(node_t[0:D, k * P:(k + 1) * P], rows_in[:, k, :], ident[:, :])
                    last.then_inc(turned[layer], 1)
                    if layer == 2:
                        pe.wait_ge(turned_copied[2], j + 2)
                        pe.wait_ge(pq_read, j + 1)
                        for k in range(BB):
                            last = mm(node_pq[:, k * 2 * D:(k + 1) * 2 * D], x_tb[b][0:D + 1, k * P:(k + 1) * P],
                                      wt("pq", D + 1), start=k in (0, 4), stop=k in (3, BB - 1),
                                      skip_group_check=True)
                        last.then_inc(pq_done, 1)
                    if layer == 3:
                        pe.wait_ge(turned_copied[3], j + 2)
                        pe.wait_ge(a_read, 3 * NBATCH + j + 1)
                        for k in range(BB):
                            last = mm(node_b[b][:, k, :], sx_t[b][0:D + 1, k * P:(k + 1) * P], wt("w4", D + 1),
                                      start=k == 0, stop=k == BB - 1, skip_group_check=True)
                        last.then_inc(y_done, 1)

                (skewed if layer == 3 else pairwise)(pe, multiply, turn)

        @block.scalar
        def _(act):
            copy = ACT.Copy
            for layer in range(4):
                act.sem_inc(turned_copied[layer], 1)
                if layer < 3:
                    act.sem_inc(counted[layer], 1)
            act.sem_inc(turn_copied, 2)
            act.sem_inc(pq_read, 1)
            act.wait_ge(w23_mm, 1)
            nc.scalar.activation(w23[:, :], pair[0][0:D + 1, 0:D], copy).then_inc(w23_ready, 1)
            act.wait_ge(cleared, 7)
            act.wait_ge(ld_w, 4 * COLS)
            act.wait_ge(flag_ready, 1)
            spread = act.value_load(flag_i[0:1, 0:1], min_val=0, max_val=1)

            for layer in range(4):
                if layer < 2:
                    with act.If(spread == 0):
                        for _, i, a, n, _ in rounds(act, "C"):
                            act.wait_ge(z_used[layer], 2 * n + 4)
                            act.wait_ge(cwin_done[layer], n + 1)
                            for q in range(4):
                                last = nc.scalar.activation(counts[:, a % 2, HI[q][0] * W:HI[q][1] * W],
                                                            count_banks[q], copy)
                            last.then_inc(counted[layer], 1)
                if layer == 2:
                    with act.If(spread == 0):
                        with act.Fori(0, TRIPLES) as n:
                            act.wait_ge(z_used[2], 2 * n + 4)
                            act.wait_ge(cwin_done[2], n + 1)
                            for q in range(4):
                                last = nc.scalar.activation(weight_sums[:, HI[q][0] * W:HI[q][1] * W],
                                                            count_banks[q], copy)
                            last.then_inc(counted[2], 1)
                if layer == 3:
                    with act.If(spread == 0):
                        with act.Fori(0, NG // 2) as i:
                            for b in range(2):
                                g = 2 * i + b
                                act.wait_ge(turn_done, g + 1)
                                act.wait_ge(zed_done, g + 1)
                                nc.scalar.activation(onehot_t[:, b, :], oh_t[b], copy).then_inc(turn_copied, 1)
                                act.wait_ge(z_summed, g + 3)
                                nc.scalar.activation(act_in[:, b, :, :], act_in[:, b, :, :], ACT.Silu)\
                                    .then_inc(silu_done, 1)
                    with act.Else():
                        with act.Fori(0, NG) as g:
                            act.wait_ge(g_sum, g + 2)
                            nc.scalar.activation(act_in[:, 0, :, :], act_in[:, 0, :, :], ACT.Silu).then_inc(g_silu, 1)

                def stage(j, b, i):
                    act.wait_ge(products[layer], j + 1)
                    act.nop(nofuse=True)
                    if layer in (0, 3):
                        nc.scalar.activation(x_tb[b][0:D, :], XT[:, bass.ds(j * BN, BN)], copy)
                    nc.scalar.activation(s_t[b][0:READ[layer], :], accT[0:READ[layer], bass.ds(j * BN, BN)], copy)\
                        .then_inc(staged[layer], 1)

                def bring(j, b, i):
                    if layer == 3:
                        act.wait_ge(products[3], j + 3)
                        act.wait_ge(y_done, j + 1)
                        nc.scalar.activation(u[b][:, :, :], node_a[b][:, :, 0:D], ACT.Silu).then_inc(u_done, 1)
                    act.wait_ge(turned[layer], j + 3)
                    act.nop(nofuse=True)
                    if layer < 2:
                        nc.scalar.activation(accT[0:D, bass.ds(j * BN, BN)], node_t[0:D, 0:BN], copy)\
                            .then_inc(turned_copied[layer], 1)
                    elif layer == 2:
                        act.wait_ge(pq_done, j + 1)
                        act.nop(nofuse=True)
                        nc.scalar.activation(XT[:, bass.ds(j * BN, BN)], node_t[0:D, 0:BN], copy)
                        nc.scalar.activation(x_tb[b][0:D, :], node_t[0:D, 0:BN], copy).then_inc(turned_copied[2], 1)
                        act.wait_ge(pq_done, j + 3)
                        act.wait_ge(slot_stored[3], j + 1)
                        pq = node_pq[:, 0:BB * 2 * D].rearrange("p (k c) -> p k c", k=BB)
                        nc.scalar.activation(tab[b][:, :, :], pq[:, :, 0:D], copy)
                        nc.scalar.activation(q_f[b][:, :, :], pq[:, :, D:2 * D], copy).then_inc(pq_read, 1)
                    else:
                        nc.scalar.activation(sx_t[b][0:D, :], node_t[0:D, 0:BN], copy).then_inc(turned_copied[3], 1)

                act.wait_ge(pass_done, layer + 1)
                (skewed if layer == 3 else pairwise)(act, stage, bring)

        @block.vector
        def _(dve):
            v = nc.vector
            tt, ts, stt = v.tensor_tensor, v.tensor_scalar, v.scalar_tensor_tensor
            link = Chain(dve, dve_step)
            for layer in range(4):
                dve.sem_inc(acc_added[layer], 2)
                if layer < 3:
                    dve.sem_inc(c_added[layer], 2 if layer < 2 else 1)
                dve.sem_inc(g_free[layer], 1)
            dve.sem_inc(batch_done[3], 2)
            dve.sem_inc(a_read, 2)
            dve.sem_inc(z_summed, 2)
            dve.sem_inc(g_sum, 1)

            for b in range(2):
                v.memset(x_tb[b][D:D + 1, :], 1.0).then_inc(cleared, 1)
                v.memset(sx_t[b][D:D + 1, :], 1.0).then_inc(cleared, 1)
            dve.wait_ge(consts, 10)
            scratch = dst_rel[:, :].bitcast(I32)
            dve.wait_ge(ld_src, COLS)
            link(ts(scratch, edge_i[:, :], P - 1, None, ALU.bitwise_and))
            link(v.tensor_copy(src_lo[:, :], scratch))
            link(ts(scratch, edge_i[:, :], 7, None, ALU.logical_shift_right))
            v.tensor_copy(src_hi[:, :], scratch).then_inc(src_split, 1)
            dve.wait_ge(src_split, 1)
            with dve.Fori(0, NG // 2) as i:
                for b in range(2):
                    g = 2 * i + b
                    dve.wait_ge(hist_mm, g + 1)
                    tt(hist_lo[:, b, :, :], iota_t[:, :, :], across(src_lo, g, P), ALU.is_equal)
                    tt(hist_hi[:, b, :, :], iota_t[:, 0:NB, :], across(src_hi, g, NB), ALU.is_equal)\
                        .then_inc(hist_oh, 1)
            dve.wait_ge(hist_mm, NG + 3)
            ts(r_out[:, :], hist, 1.0, None, ALU.max).then_inc(asked, 1)
            dve.wait_ge(rooted, 1)
            dve.wait_ge(ld_x, COLS)
            tt(X0, X[:, :, :], along(r_out[:, :], D), ALU.mult).then_inc(t0_ready, 1)
            dve.wait_ge(ld_first, 2 * COLS)
            link(v.tensor_copy(first_f[:, :], first_bc[:, :]))
            dve.wait_ge(ld_dst, COLS)
            link(v.tensor_copy(dst_rel[:, :], edge_i[:, :]))
            rel3 = dst_rel[:, :].rearrange("p (g t) -> p g t", t=TG)
            link(tt(rel3, rel3, along(first_f[:, :], TG), ALU.subtract))
            share3 = comb.rearrange("p (g t) -> p g t", t=TG)
            for t in range(TG):
                link(ts(share3[:, :, t], rel3[:, :, t], float(-SHARE[t]), None, ALU.add))
            link(tt(tile_steps.rearrange("p (g t) -> p g t", t=TG - 1), rel3[:, :, 1:TG], rel3[:, :, 0:TG - 1],
                    ALU.subtract))
            link(v.tensor_reduce(span[:, 2:3], tile_steps, AX.X, ALU.min))
            link(v.tensor_reduce(span[:, 0:1], comb, AX.X, ALU.max))
            link(v.tensor_reduce(span[:, 1:2], comb, AX.X, ALU.min))
            link(ts(span[:, 0:1], span[:, 0:1], float(1 - WS), None, ALU.add))
            link(stt(span[:, 1:2], span[:, 2:3], -1.0, span[:, 1:2], ALU.add, ALU.min))
            stt(span[:, 3:4], span[:, 1:2], -1.0, span[:, 0:1], ALU.mult, ALU.max).then_inc(span_ready, 1)
            link(stt(comb, src_hi[:, :], float(WS), comb, ALU.mult, ALU.add))
            dve.wait_ge(span_turned, 1)
            link(v.tensor_reduce(flag_f[:, 0:1], pair[1][0:1, 0:P], AX.X, ALU.max))
            link(ts(flag_f[:, 1:2], flag_f[:, 0:1], 0.0, None, ALU.is_gt))
            v.tensor_copy(flag_i[:, :], flag_f[:, 1:2]).then_inc(flag_ready, 1)
            dve.wait_ge(t0_ready, 1)
            link(v.tensor_copy(xparts[:, :, 0:D], X0))
            dve.wait_ge(stored[0][0], COLS)
            link(tt(X0, X0, xparts[:, :, 0:D], ALU.subtract))
            link(v.tensor_copy(xparts[:, :, D:2 * D], X0))
            link(tt(X0, X0, xparts[:, :, D:2 * D], ALU.subtract))
            v.tensor_copy(xparts[:, :, 2 * D:3 * D], X0).then_inc(parts_ready, 1)
            dve.wait_ge(parts_ready, 1)
            dve.wait_ge(ld_w, 4 * COLS)
            dve.wait_ge(cleared, 7)
            dve.wait_ge(flag_ready, 1)
            link.close()
            spread = dve.value_load(flag_i[0:1, 0:1], min_val=0, max_val=1)

            def norm(to, x, eps, n, done=None, free=None):
                two(lambda b: v.tensor_reduce(c1[b][:, :], x(b), AX.X, ALU.add))
                two(lambda b: stt(t1[b][:, :, :], along(c1[b][:, :], D), -1.0 / D, x(b), ALU.mult, ALU.add))
                two(lambda b: tt(t2[b][:, :, :], t1[b][:, :, :], t1[b][:, :, :], ALU.mult))
                two(lambda b: v.tensor_reduce(c1[b][:, :], t2[b][:, :, :], AX.X, ALU.add))
                for b in range(2):
                    link.wait_own(b)
                    ts(c2[b][:, 0, :], c1[b][:, :], 1.0 / D, float(eps), ALU.mult, ALU.add).then_inc(asked, 1)
                for b in range(2):
                    if free is not None:
                        free(b)
                    dve.wait_ge(rooted, n + b)
                    tt(to(b), t1[b][:, :, :], along(c3[b][:, 0, :], D), ALU.mult).then_inc(done or normed, 1)

            for layer in range(4):
                m = SUMS[layer]
                if layer == 3:
                    for b in range(2):
                        v.memset(sx_t[b][D:D + 1, :], 1.0).then_inc(cleared, 1)
                    dve.wait_ge(cleared, 10)
                elif layer > 0:
                    dve.wait_ge(turned_copied[layer - 1], NBATCH + 1)
                with dve.If(spread == 0):
                    def add_window(g, bank_):
                        first = dve.value_load(first_i[0:1, bass.ds(g, 1)], min_val=0, max_val=NP - W)
                        sums = accT[0:m, bass.ds(first, W)]
                        return lambda: tt(sums, sums, bank_[0:m, :], ALU.add)

                    def mark_sources(n, b, g):
                        dve.wait_ge(z_used[layer], 2 * n + 1)
                        tt(hist_lo[:, b, :, :], iota_t[:, :, :], across(src_lo, g, P), ALU.is_equal)
                        for t in range(TG):
                            if t % HALF == 0:
                                dve.wait_ge(z_used[layer], 2 * n + t // HALF + 1)
                            last = ts(zrows[:, t, 0:NH * WS], iota_z[:, :], comb[:, bass.ds(g * TG + t, 1)],
                                      None, ALU.is_equal)
                            if t % HALF == HALF - 1:
                                last.then_inc(z_ready[layer], 1)

                    def mark_targets(n, b, g):
                        dve.wait_ge(win_done[layer], n + 1)
                        last = tt(onehot[:, b, :, :], iota_bc(W), along(cols(dst_rel, g), W), ALU.is_equal)
                        if layer == 0:
                            last = v.tensor_copy(msg[:, b, :, D + 1], cols(weight_cols, g))
                        last.then_inc(oh_ready[layer], 1)

                    def mark_counted_targets(n, b, g):
                        if layer == 0:
                            dve.wait_ge(cwin_done[0], n + 1)
                            tt(onehot_c[:, b, :, :], iota_bc(W), along(cols(dst_rel, g), W), ALU.is_equal)
                            v.tensor_copy(ones_w[:, b, :, D + 1], cols(weight_cols, g)).then_inc(ones_ready, 1)

                    def after_last(kind, n_g, n_c):
                        if kind == "G":
                            dve.wait_ge(acc_added[layer], n_g + 2)
                        else:
                            dve.wait_ge(c_added[layer], n_c + 2)

                    def add_gathered_window(n, b, g, before, n_c):
                        add = add_window(g, win[b])
                        dve.wait_ge(win_done[layer], n + 3)
                        after_last(before, n, n_c)
                        add().then_inc(acc_added[layer], 1)

                    def add_counted_window(n, b, g, before, n_g):
                        first = dve.value_load(first_i[0:1, bass.ds(g, 1)], min_val=0, max_val=NP - W)
                        sums = accT[0:m, bass.ds(first, W)]
                        parts = accT[0:D, bass.ds(first, W)]
                        dve.wait_ge(cwin_done[layer], n + 3)
                        after_last(before, n_g, n)
                        tt(sums, sums, cwin_c[b][0:m, :], ALU.add).then_inc(c_part, 1)
                        dve.wait_ge(c_part, 2 * (layer * N_OF["C"] + n) + 1)
                        tt(parts, parts, cwin_ab[b][D:2 * D, :], ALU.add).then_inc(c_part, 1)
                        dve.wait_ge(c_part, 2 * (layer * N_OF["C"] + n) + 2)
                        tt(parts, parts, cwin_ab[b][0:D, :], ALU.add).then_inc(c_added[layer], 1)

                    if layer < 2:
                        for b in range(2):
                            mark_sources(b, b, group_of("C", 0, b))
                            mark_targets(b, b, group_of("G", 0, b))
                            mark_counted_targets(b, b, group_of("C", 0, b))
                        before = PATTERN[-1]
                        for kind, i, a, n, tail in rounds(dve):
                            b, g, ahead = a % 2, group_of(kind, i, a), not tail or a + 2 < TAILS[kind]
                            other = i * len(PLACES["C" if kind == "G" else "G"]) + \
                                sum(x != kind for x in PATTERN[:PLACES[kind][a]])
                            if kind == "G":
                                add_gathered_window(n, b, g, before, other)
                                if ahead:
                                    mark_targets(n + 2, b, group_of("G", i, a + 2))
                            else:
                                if ahead:
                                    mark_sources(n + 2, b, group_of("C", i, a + 2))
                                add_counted_window(n, b, g, before, other)
                                if ahead:
                                    mark_counted_targets(n + 2, b, group_of("C", i, a + 2))
                            before = kind
                        dve.wait_ge(c_added[layer], N_OF["C"] + 2)
                        dve.wait_ge(acc_added[layer], N_OF["G"] + 2)
                    if layer == 2:
                        def weigh_sources(n):
                            g = 3 * n + 2
                            dve.wait_ge(z_used[2], 2 * n + 2)
                            v.tensor_copy(lo_f[:, :], cols(src_lo, g))
                            v.tensor_copy(w_part[:, 0, :], cols(weight_cols, g)).then_inc(w_split, 1)
                            dve.wait_ge(w_split, 4 * n + 1)
                            tt(w_rest[:, 0, :], cols(weight_cols, g), w_part[:, 0, :], ALU.subtract)\
                                .then_inc(w_split, 1)
                            dve.wait_ge(w_split, 4 * n + 2)
                            v.tensor_copy(w_part[:, 1, :], w_rest[:, 0, :]).then_inc(w_split, 1)
                            dve.wait_ge(w_split, 4 * n + 3)
                            tt(w_rest[:, 1, :], w_rest[:, 0, :], w_part[:, 1, :], ALU.subtract).then_inc(w_split, 1)
                            dve.wait_ge(w_split, 4 * n + 4)
                            for t in range(TG):
                                for p, weight in enumerate((weight_cols[:, bass.ds(g * TG + t, 1)],
                                                            w_rest[:, 0, t:t + 1], w_rest[:, 1, t:t + 1])):
                                    ts(lo_w[:, t, p, :], iota_z[:, 0:P], lo_f[:, t:t + 1], weight, ALU.is_equal,
                                       ALU.mult)
                                last = ts(zrows[:, t, 0:NH * WS], iota_z[:, :], comb[:, bass.ds(g * TG + t, 1)],
                                          None, ALU.is_equal)
                                if t % HALF == HALF - 1:
                                    last.then_inc(z_ready[2], 1)

                        def mark_weights(n, s):
                            at = 2 * n + s
                            dve.wait_ge(win_done[2], at + 1)
                            tt(onehot[:, s, :, :], iota_bc(W), along(cols(dst_rel, 3 * n + s), W), ALU.is_equal)\
                                .then_inc(oh_raw, 1)
                            dve.wait_ge(oh_raw, at + 1)
                            tt(onehot[:, s, :, :], onehot[:, s, :, :], along(cols(weight_cols, 3 * n + s), W),
                               ALU.mult).then_inc(oh_ready[2], 1)

                        def add_gathered(n, s):
                            add = add_window(3 * n + s, win[s])
                            dve.wait_ge(win_done[2], 2 * n + s + 3)
                            dve.wait_ge(c_added[2], n + 1)
                            dve.wait_ge(acc_added[2], 2 * n + s + 2)
                            add().then_inc(acc_added[2], 1)

                        def add_counted(n):
                            add = add_window(3 * n + 2, cwin_ab[0])
                            dve.wait_ge(cwin_done[2], n + 2)
                            dve.wait_ge(acc_added[2], 2 * n + 4)
                            add().then_inc(c_added[2], 1)

                        weigh_sources(0)
                        mark_weights(0, 0)
                        weigh_sources(1)
                        mark_weights(0, 1)
                        add_gathered(0, 0)
                        mark_weights(1, 0)
                        with dve.Fori(0, TRIPLES - 2) as n:
                            weigh_sources(n + 2)
                            add_gathered(n, 1)
                            add_counted(n)
                            mark_weights(n + 1, 1)
                            add_gathered(n + 1, 0)
                            mark_weights(n + 2, 0)
                        add_gathered(TRIPLES - 2, 1)
                        add_counted(TRIPLES - 2)
                        mark_weights(TRIPLES - 1, 1)
                        add_gathered(TRIPLES - 1, 0)
                        if REST > 0:
                            mark_weights(TRIPLES, 0)
                        add_gathered(TRIPLES - 1, 1)
                        add_counted(TRIPLES - 1)
                        if REST > 1:
                            mark_weights(TRIPLES, 1)
                        for s in range(REST):
                            add_gathered(TRIPLES, s)
                        dve.wait_ge(c_added[2], TRIPLES + 1)
                        dve.wait_ge(acc_added[2], 2 * TRIPLES + REST + 2)
                    for i in two_by_two(dve, layer):
                        for b in range(2):
                            g = 2 * i + b
                            dve.wait_ge(win_done[3], g + 1)
                            tt(onehot16[:, b, :, :], iota_bc(W), along(cols(dst_rel, g), W), ALU.is_equal)
                            tt(onehot[:, b, :, :], iota_bc(W), along(cols(dst_rel, g), W), ALU.is_equal)\
                                .then_inc(oh_ready[3], 1)
                            dve.wait_ge(gathered[3][b], (i + 1) * COLS * TG)
                            dve.wait_ge(zed_done, g + 3)
                            tt(act_in[:, b, :, :], zed[b], msg[:, b, :, 0:D], ALU.add).then_inc(z_summed, 1)
                            add = add_window(g, win[b])
                            dve.wait_ge(win_done[3], g + 3)
                            dve.wait_ge(acc_added[3], g + 2)
                            add().then_inc(acc_added[3], 1)
                    if layer == 3:
                        dve.wait_ge(acc_added[3], NG + 2)
                with dve.Else():
                    with dve.Fori(0, NG) as g:
                        if layer == 0:
                            v.tensor_copy(msg[:, 0, :, D + 1], cols(weight_cols, g))
                        if layer == 3:
                            dve.wait_ge(g_gathered[3], (g + 1) * COLS * 2 * TG)
                            dve.wait_ge(g_zed, g + 2)
                            tt(act_in[:, 0, :, :], zed[0], msg[:, 0, :, 0:D], ALU.add).then_inc(g_part, 1)
                            dve.wait_ge(g_part, g + 1)
                            tt(act_in[:, 0, :, :], act_in[:, 0, :, :], q_rows[:, :, :], ALU.add).then_inc(g_sum, 1)
                        tt(rel_w[:, :], cols(dst_rel, g), first_f[:, bass.ds(g, 1)].broadcast_to((P, TG)), ALU.add)\
                            .then_inc(g_rel[layer], 1)
                        with dve.Fori(0, NW) as w:
                            n = g * NW + w
                            dve.wait_ge(g_rel[layer], n + g + 1)
                            tt(onehot[:, 0, :, :], iota_bc(W), along(rel_w[:, :], W), ALU.is_equal)\
                                .then_inc(g_raw if layer == 2 else g_oh[layer], 1)
                            if layer == 2:
                                dve.wait_ge(g_raw, n + 1)
                                tt(onehot[:, 0, :, :], onehot[:, 0, :, :], along(cols(weight_cols, g), W), ALU.mult)\
                                    .then_inc(g_oh[2], 1)
                            sums = accT[0:m, bass.ds(w * W, W)]
                            dve.wait_ge(g_win[layer], n + 1)
                            ts(rel_w[:, :], rel_w[:, :], float(-W), None, ALU.add).then_inc(g_rel[layer], 1)
                            tt(sums, sums, win[0][0:m, :], ALU.add).then_inc(g_added[layer], 1)
                            dve.wait_ge(g_added[layer], n + 1)
                        dve.sem_inc(g_free[layer], 1)
                dve.sem_inc(pass_done, 1)

                roots = ROOTS_BEFORE[layer]
                norms_before = (0, 2, 6, 8)[layer] * (NBATCH // 2)
                steps = {0: 14, 1: 26, 2: 12, 3: 22}[layer]
                two = link.two

                def multiply_sums(j, b):
                    dve.wait_ge(staged[0], j + 1)
                    tt(sx_t[b][0:D + 1, :], s_t[b][0:D + 1, :], x_tb[b][0:D + 1, :], ALU.mult).then_inc(sx_ready, 1)

                def batches(i, more=True):
                    def j(b):
                        return 2 * i + b

                    def at(b):
                        return bass.ds(j(b) * BB, BB)

                    def A(b):
                        return node_a[b][:, :, 0:D]

                    def Xb(b):
                        return X[:, at(b), :]

                    def read_sums(step):
                        for b in range(2):
                            if link.n > 0:
                                link.wait_own(b)
                            step(b).then_inc(a_read, 1)
                        dve.wait_ge(a_read, layer * NBATCH + j(1) + 3)

                    def norm_done(k):
                        dve.wait_ge(normed, norms_before + (4 if layer == 1 else 2) * i + k)

                    if layer == 0:
                        for b in range(2):
                            dve.wait_ge(products[0], j(b) + 3)
                            ts(c2[b][:, 0, :], node_a[b][:, :, D], 1.0, None, ALU.max)
                            ts(c2[b][:, 1, :], node_a[b][:, :, D], 1.0, None, ALU.add).then_inc(asked, 1)
                            v.tensor_copy(degrees[:, at(b), :], node_a[b][:, :, D:D + 2])
                        if more:
                            for b in range(2):
                                multiply_sums(j(b) + 2, b)
                        dve.wait_ge(rooted, roots + 4 * i + 2)
                        two(lambda b: tt(t1[b][:, :, :], A(b), along(c3[b][:, 0, :], D), ALU.mult))
                        two(lambda b: v.tensor_copy(dinv1[:, at(b)], c3[b][:, 1, :]))
                        read_sums(lambda b: tt(t1[b][:, :, :], t1[b][:, :, :], node_b[b], ALU.add))
                        two(lambda b: tt(t2[b][:, :, :], t1[b][:, :, :], Xb(b), ALU.add))
                        norm(Xb, lambda b: t2[b][:, :, :], 1e-5, roots + 4 * i + 3)
                        norm_done(2)
                        for b in range(2):
                            dve.wait_ge(slot_stored[1], j(b) + 1)
                            dve.wait_ge(split_done[0], j(b) + 1)
                            dve.wait_ge(turned[0], j(b) + 1)
                            tt(tab[b][:, :, :], Xb(b), along(dinv1[:, at(b)], D), ALU.mult).then_inc(batch_done[0], 1)
                    elif layer == 1:
                        dve.wait_ge(products[1], j(1) + 3)
                        read_sums(lambda b: tt(t1[b][:, :, :], A(b), along(dinv1[:, at(b)], D), ALU.mult))
                        two(lambda b: tt(t1[b][:, :, :], t1[b][:, :, :], row("b1"), ALU.add))
                        two(lambda b: stt(t1[b][:, :, :], t1[b][:, :, :], 0.0, Xb(b), ALU.max, ALU.add))
                        norm(lambda b: t2[b][:, :, :], lambda b: t1[b][:, :, :], 1e-8, roots + 4 * i + 1)
                        norm_done(2)
                        two(lambda b: tt(t2[b][:, :, :], t2[b][:, :, :], row("gamma1"), ALU.mult))
                        two(lambda b: tt(t2[b][:, :, :], t2[b][:, :, :], row("beta1"), ALU.add))
                        two(lambda b: tt(t2[b][:, :, :], t2[b][:, :, :], Xb(b), ALU.add))
                        norm(Xb, lambda b: t2[b][:, :, :], 1e-5, roots + 4 * i + 3)
                        norm_done(4)
                        for b in range(2):
                            dve.wait_ge(slot_stored[2], j(b) + 1)
                            dve.wait_ge(split_done[1], j(b) + 1)
                            dve.wait_ge(turned[1], j(b) + 1)
                            tt(tab[b][:, :, :], Xb(b), along(dis2[:, at(b)], D), ALU.mult).then_inc(batch_done[1], 1)
                    elif layer == 2:
                        dve.wait_ge(products[2], j(1) + 3)
                        read_sums(lambda b: tt(t1[b][:, :, :], A(b), along(dis2[:, at(b)], D), ALU.mult))
                        two(lambda b: tt(t1[b][:, :, :], t1[b][:, :, :], row("b2"), ALU.add))
                        two(lambda b: stt(t1[b][:, :, :], t1[b][:, :, :], 0.0, Xb(b), ALU.max, ALU.add))
                        norm(lambda b: u[b][:, :, :], lambda b: t1[b][:, :, :], 1e-5, roots + 2 * i + 1,
                             free=lambda b: dve.wait_ge(turned[2], j(b) + 1))
                        for b in range(2):
                            tt(Xb(b), t1[b][:, :, :], along(c3[b][:, 0, :], D), ALU.mult).then_inc(batch_done[2], 1)
                        norm_done(2)
                        dve.wait_ge(batch_done[2], j(1) + 1)
                    else:
                        dve.wait_ge(y_done, j(1) + 3)
                        read_sums(lambda b: tt(t1[b][:, :, :], node_b[b], Xb(b), ALU.add))
                        norm(lambda b: t2[b][:, :, :], lambda b: t1[b][:, :, :], 1e-5, roots + 4 * i + 1)
                        norm_done(2)
                        two(lambda b: tt(t2[b][:, :, :], t2[b][:, :, :], row("gamma3"), ALU.mult))
                        two(lambda b: tt(t2[b][:, :, :], t2[b][:, :, :], row("beta3"), ALU.add))
                        two(lambda b: tt(t2[b][:, :, :], t2[b][:, :, :], Xb(b), ALU.add))
                        norm(lambda b: tab[b][:, :, :], lambda b: t2[b][:, :, :], 1e-5, roots + 4 * i + 3,
                             batch_done[3], lambda b: dve.wait_ge(slot_stored[4], j(b) + 1))
                        dve.wait_ge(batch_done[3], j(1) + 3)

                loops = NBATCH // 2 - (layer == 0)
                if layer == 0:
                    for b in range(2):
                        multiply_sums(b, b)
                with dve.Fori(0, loops) as i:
                    link.enter(i, steps)
                    batches(i)
                    link.wait_own(1)
                link.leave(loops)
                if layer == 0:
                    batches(NBATCH // 2 - 1, more=False)
                    link.wait_own(1)
                    link.close()
                if layer == 0:
                    link(ts(dis_a[:, :], degrees[:, :, 1], 1.0, None, ALU.add))
                    link(ts(dis_b[:, :], dis_a[:, :], 0.0, None, ALU.is_gt))
                    ts(dis_a[:, :], dis_a[:, :], TINY, None, ALU.max).then_inc(asked, 1)
                    dve.wait_ge(rooted, ROOTS_BEFORE[1])
                    link(tt(dis2[:, :], dis_a[:, :], dis_b[:, :], ALU.mult))
                    link.close()


def kernel(**inputs):
    import numpy as _np
    import concourse.bacc as _bacc
    from concourse import mybir as _mybir
    from concourse.bass_utils import run_bass_kernel_spmd as _run

    a = {name: _np.ascontiguousarray(x) for name, x in inputs.items()}
    n, e = a["x"].shape[0], a["src"].shape[0]
    n_pad, e_pad = shapes(n, e)
    NB, NG, f = n_pad // P, e_pad // GE, a["x"].dtype

    def edges(x, fill):
        full = _np.empty((e_pad,), x.dtype)
        full[:e] = x
        full[e:] = fill
        return _np.ascontiguousarray(full.reshape(NG * TG, P).T), full

    src_cols, _ = edges(a["src"], n)
    dst_cols, dst_full = edges(a["dst"], n + _np.arange(e_pad - e) * n // e)
    w_cols, _ = edges(a["edge_weight"], 0)
    dst_first = _np.ascontiguousarray(_np.broadcast_to(dst_full[::GE], (P, NG)))
    x_full = _np.zeros((n_pad, D), f)
    x_full[:n] = a["x"]
    x_nodes = _np.ascontiguousarray(x_full.reshape(NB, P, D).transpose(1, 0, 2))
    x_t = _np.ascontiguousarray(x_full.T)
    edge_full = _np.zeros((e_pad, DE), f)
    edge_full[:e] = a["edge_attr_32"]
    edge_t = _np.ascontiguousarray(edge_full.reshape(NG, 2, 4, P, DE).transpose(2, 4, 0, 1, 3).reshape(P, NG * 2, P))

    weights = _np.zeros((P, WCOLS), f)

    def put(name, at_row, at_col, x):
        at = WEIGHTS[name][0] + at_col
        weights[at_row:at_row + x.shape[0], at:at + x.shape[1]] = x

    one = _np.ones((1, 1), f)
    w1, w3 = a["L3_gnn_w1"], a["L3_gnn_w3"]
    for k in range(4):
        put("edge", k * DE, k * D, w1[2 * D:])
    put("wn", 0, 0, a["L0_gnn_Wn"].T)
    put("wn", D, 0, a["L0_gnn_bn"][None])
    put("wn", D, D, one)
    put("wn", D + 1, D + 1, one)
    put("wm", 0, 0, a["L0_gnn_Wm"].T)
    put("wm", D, 0, a["L0_gnn_bm"][None])
    put("xn", 0, 0, a["L0_gnn_Wn"].T)
    put("xn", D, 0, a["L0_gnn_bn"][None])
    put("w1", 0, 0, a["L1_gnn_W"])
    put("w2", 0, 0, a["L2_gnn_W"].T)
    put("pq", 0, 0, w1[:D])
    put("pq", D, 0, a["L3_gnn_b1"][None])
    put("pq", 0, D, w1[D:2 * D])
    put("w2t_b2", 0, 0, a["L3_gnn_w2"].T)
    put("w2t_b2", 0, D, a["L3_gnn_b2"][:, None])
    put("w3b", 0, 0, w3[D:])
    put("w3a", 0, 0, w3[:D])
    put("w3a", D, 0, a["L3_gnn_b3"][None])
    put("w4", 0, 0, a["L3_gnn_w4"])
    put("w4", D, 0, a["L3_gnn_b4"][None])
    rows = _np.stack([a[k] for k in ("L1_gnn_b", "L1_gnn_ln_gamma", "L1_gnn_ln_beta", "L2_gnn_b", "L3_gnn_gamma",
                                     "L3_gnn_beta")])
    rows = _np.ascontiguousarray(_np.broadcast_to(rows, (P,) + rows.shape))

    nc = _bacc.Bacc("TRN2", target_bir_lowering=False, num_devices=1)
    arrays, args = {}, []
    for name, x in (("x_nodes", x_nodes), ("x_t", x_t), ("src_cols", src_cols), ("dst_cols", dst_cols),
                    ("dst_first", dst_first), ("w_cols", w_cols), ("edge_t", edge_t), ("weights", weights),
                    ("rows", rows)):
        arrays[f"in_{name}"] = x
        args.append(nc.dram_tensor(f"in_{name}", x.shape, _mybir.dt.from_np(x.dtype), kind="ExternalInput").ap())
    args.append(nc.dram_tensor("out_nodes", (P, NB, D), _mybir.dt.from_np(f), kind="ExternalOutput").ap())
    gnn_program(nc, *args, n, e)
    r = _run(nc, [arrays], core_ids=[0])
    return _np.ascontiguousarray(r.results[0]["out_nodes"].transpose(1, 0, 2).reshape(n_pad, D)[:n])
```
